# Optimizing a Trainium2 kernel written in Bass

```python
import numpy as np
import jax
import jax.numpy as jnp

def _softmax(x, axis=-1):
    return jax.nn.softmax(x, axis=axis)

def _gelu(x):
    return jax.nn.gelu(x, approximate=True)

def _silu(x):
    return jax.nn.silu(x)

def _sigmoid(x):
    return jax.nn.sigmoid(x)

def _layernorm(x, axis=-1, eps=1e-05):
    m = jnp.mean(x, axis=axis, keepdims=True)
    v = jnp.var(x, axis=axis, keepdims=True)
    return (x - m) / jnp.sqrt(v + eps)

def _scatter_add(tgt, idx, src, axis=0):
    return tgt.at[idx].add(src)

def _segment_sum(src, seg, n):
    return jax.ops.segment_sum(src, seg, n)
kernel_name = 'mk_xattn_ffn_d1_seqx_r4_08d96b'

def setup_inputs(seed: int=0):
    np.random.seed(seed)
    _w = jnp.asarray

    def _rec_inputs():
        import jax
        import jax.numpy as jnp
        _rk = jax.random.key(seed)
        x = 7.22e-05 + 1 * jax.random.normal(jax.random.fold_in(_rk, 1), (16, 256, 256), jnp.float32)
        _lenS = 256 - jax.random.randint(jax.random.fold_in(_rk, 7), (16,), 0, max(1, 256 // 4) + 1, jnp.int32)
        _lenS2 = 256 - jax.random.randint(jax.random.fold_in(_rk, 8), (16,), 0, max(1, 256 // 4) + 1, jnp.int32)
        _ctx_1024P = jax.random.normal(jax.random.fold_in(_rk, 11), (16, 16, 256), jnp.float32)
        _ctx_1024c = jax.random.dirichlet(jax.random.fold_in(_rk, 511), 0.3 * jnp.ones((16,), jnp.float32), (16, 256))
        _ctx_1024t = jnp.einsum('bsk,bkd->bsd', _ctx_1024c, _ctx_1024P)
        _ctx_1024t = _ctx_1024t * jax.lax.rsqrt(jnp.mean(jnp.square(_ctx_1024t)) + 1e-12) * 0.953939
        ctx_1024 = 4.13588e-05 + 0.999923 * (_ctx_1024t + 0.3 * jax.random.normal(jax.random.fold_in(_rk, 611), (16, 256, 256), jnp.float32))
        return (x, ctx_1024)
    x, ctx_1024 = _rec_inputs()

    def _L0_xattn_setup():
        import jax, jax.numpy as jnp
        import numpy as np
        N_HEADS = 16
        D_MODEL = 256
        D_K = D_MODEL // N_HEADS
        key = jax.random.key(seed)
        ks = jax.random.split(key, 7)
        b, n = (4, 512)
        s = 0.02
        return {'Q': jax.random.normal(ks[0], (b, n, D_MODEL), jnp.float32), 'K': jax.random.normal(ks[1], (b, n, D_MODEL), jnp.float32), 'V': jax.random.normal(ks[2], (b, n, D_MODEL), jnp.float32), 'w_q': jax.random.normal(ks[3], (D_MODEL, D_MODEL), jnp.float32) * s, 'w_k': jax.random.normal(ks[4], (D_MODEL, D_MODEL), jnp.float32) * s, 'w_v': jax.random.normal(ks[5], (D_MODEL, D_MODEL), jnp.float32) * s, 'w_o': jax.random.normal(ks[6], (D_MODEL, D_MODEL), jnp.float32) * s}
    _L0_xattn_all = _L0_xattn_setup()
    _L0_xattn_in = {k: v for k, v in _L0_xattn_all.items() if k in ('w_q', 'w_k', 'w_v', 'w_o')}
    del _L0_xattn_all

    def _L0_ffn_setup():
        import jax, jax.numpy as jnp
        import numpy as np
        LATENT = 256
        LEAF_W = 64
        DEPTH = 4
        N_LEAVES = 2 ** DEPTH
        N_NODES = 2 ** DEPTH - 1
        B, S = (4, 512)

        def _fff_params(key, prefix):
            ks = jax.random.split(key, 4)
            d, h, l, n = (LATENT, LEAF_W, N_LEAVES, N_NODES)
            s_in = 1.0 / np.sqrt(d).astype(np.float32)
            s_h = 1.0 / np.sqrt(h).astype(np.float32)
            return {f'{prefix}_node_w': jax.random.normal(ks[0], (n, d), jnp.float32) * s_in, f'{prefix}_node_b': jax.random.normal(ks[1], (n,), jnp.float32) * s_in, f'{prefix}_w1': jax.random.normal(ks[2], (l, d, h), jnp.float32) * s_in, f'{prefix}_b1': jnp.zeros((l, h), jnp.float32), f'{prefix}_w2': jax.random.normal(ks[3], (l, h, d), jnp.float32) * s_h, f'{prefix}_b2': jnp.zeros((l, d), jnp.float32)}

        def _fff(x, node_w, node_b, w1, b1, w2, b2):
            Bx, Sx, D = x.shape
            xf = x.reshape(-1, D)
            N = xf.shape[0]
            cur = jnp.zeros((N,), jnp.int32)
            for _ in range(DEPTH):
                pw = node_w[cur]
                score = jnp.einsum('nd,nd->n', xf, pw) + node_b[cur]
                cur = 2 * cur + 1 + (score >= 0).astype(jnp.int32)
            leaf = cur - N_NODES
            sel = jax.nn.one_hot(leaf, N_LEAVES, dtype=xf.dtype)
            hidden_all = jax.nn.relu(jnp.einsum('nd,ldh->lnh', xf, w1) + b1[:, None, :])
            hidden = hidden_all * sel.T[:, :, None]
            out = jnp.einsum('lnh,lho->no', hidden, w2) + sel @ b2
            return out.reshape(Bx, Sx, D)
        key = jax.random.key(seed)
        kx, kq, kk, kv = jax.random.split(key, 4)
        inp = {'x': jax.random.normal(kx, (B, S, LATENT), jnp.float32)}
        inp.update(_fff_params(kq, 'q'))
        inp.update(_fff_params(kk, 'k'))
        inp.update(_fff_params(kv, 'v'))
        return inp
    _L0_ffn_all = _L0_ffn_setup()
    _L0_ffn_in = {k: v for k, v in _L0_ffn_all.items() if k in ('q_node_w', 'q_node_b', 'q_w1', 'q_b1', 'q_w2', 'q_b2', 'k_node_w', 'k_node_b', 'k_w1', 'k_b1', 'k_w2', 'k_b2', 'v_node_w', 'v_node_b', 'v_w1', 'v_b1', 'v_w2', 'v_b2')}
    del _L0_ffn_all
    return {'x': x, 'ctx_1024': ctx_1024, 'L0_xattn_w_q': _L0_xattn_in['w_q'], 'L0_xattn_w_k': _L0_xattn_in['w_k'], 'L0_xattn_w_v': _L0_xattn_in['w_v'], 'L0_xattn_w_o': _L0_xattn_in['w_o'], 'L0_ffn_q_node_w': _L0_ffn_in['q_node_w'], 'L0_ffn_q_node_b': _L0_ffn_in['q_node_b'], 'L0_ffn_q_w1': _L0_ffn_in['q_w1'], 'L0_ffn_q_b1': _L0_ffn_in['q_b1'], 'L0_ffn_q_w2': _L0_ffn_in['q_w2'], 'L0_ffn_q_b2': _L0_ffn_in['q_b2'], 'L0_ffn_k_node_w': _L0_ffn_in['k_node_w'], 'L0_ffn_k_node_b': _L0_ffn_in['k_node_b'], 'L0_ffn_k_w1': _L0_ffn_in['k_w1'], 'L0_ffn_k_b1': _L0_ffn_in['k_b1'], 'L0_ffn_k_w2': _L0_ffn_in['k_w2'], 'L0_ffn_k_b2': _L0_ffn_in['k_b2'], 'L0_ffn_v_node_w': _L0_ffn_in['v_node_w'], 'L0_ffn_v_node_b': _L0_ffn_in['v_node_b'], 'L0_ffn_v_w1': _L0_ffn_in['v_w1'], 'L0_ffn_v_b1': _L0_ffn_in['v_b1'], 'L0_ffn_v_w2': _L0_ffn_in['v_w2'], 'L0_ffn_v_b2': _L0_ffn_in['v_b2']}

def reference(x, ctx_1024, L0_xattn_w_q, L0_xattn_w_k, L0_xattn_w_v, L0_xattn_w_o, L0_ffn_q_node_w, L0_ffn_q_node_b, L0_ffn_q_w1, L0_ffn_q_b1, L0_ffn_q_w2, L0_ffn_q_b2, L0_ffn_k_node_w, L0_ffn_k_node_b, L0_ffn_k_w1, L0_ffn_k_b1, L0_ffn_k_w2, L0_ffn_k_b2, L0_ffn_v_node_w, L0_ffn_v_node_b, L0_ffn_v_w1, L0_ffn_v_b1, L0_ffn_v_w2, L0_ffn_v_b2):
    import jax
    import jax.numpy as jnp

    def _L0_xattn_ref(Q, K, V, w_q, w_k, w_v, w_o):
        import jax, jax.numpy as jnp
        import numpy as np
        N_HEADS = 16
        D_MODEL = 256
        D_K = D_MODEL // N_HEADS
        b, n, _ = Q.shape
        q = (Q @ w_q.T).reshape(b, n, N_HEADS, D_K).transpose(0, 2, 1, 3)
        k = (K @ w_k.T).reshape(b, n, N_HEADS, D_K).transpose(0, 2, 1, 3)
        v = (V @ w_v.T).reshape(b, n, N_HEADS, D_K).transpose(0, 2, 1, 3)
        scores = jnp.einsum('bhqd,bhkd->bhqk', q, k) / jnp.sqrt(jnp.float32(D_K))
        causal = jnp.tril(jnp.ones((n, n), dtype=bool))
        scores = jnp.where(causal[None, None], scores, -jnp.inf)
        weights = jax.nn.softmax(scores, axis=-1)
        attn = jnp.einsum('bhqk,bhkd->bhqd', weights, v)
        attn = attn.transpose(0, 2, 1, 3).reshape(b, n, D_MODEL)
        return attn @ w_o.T

    def _L0_ffn_ref(x, q_node_w, q_node_b, q_w1, q_b1, q_w2, q_b2, k_node_w, k_node_b, k_w1, k_b1, k_w2, k_b2, v_node_w, v_node_b, v_w1, v_b1, v_w2, v_b2):
        import jax, jax.numpy as jnp
        import numpy as np
        LATENT = 256
        LEAF_W = 64
        DEPTH = 4
        N_LEAVES = 2 ** DEPTH
        N_NODES = 2 ** DEPTH - 1
        B, S = (4, 512)

        def _fff_params(key, prefix):
            ks = jax.random.split(key, 4)
            d, h, l, n = (LATENT, LEAF_W, N_LEAVES, N_NODES)
            s_in = 1.0 / np.sqrt(d).astype(np.float32)
            s_h = 1.0 / np.sqrt(h).astype(np.float32)
            return {f'{prefix}_node_w': jax.random.normal(ks[0], (n, d), jnp.float32) * s_in, f'{prefix}_node_b': jax.random.normal(ks[1], (n,), jnp.float32) * s_in, f'{prefix}_w1': jax.random.normal(ks[2], (l, d, h), jnp.float32) * s_in, f'{prefix}_b1': jnp.zeros((l, h), jnp.float32), f'{prefix}_w2': jax.random.normal(ks[3], (l, h, d), jnp.float32) * s_h, f'{prefix}_b2': jnp.zeros((l, d), jnp.float32)}

        def _fff(x, node_w, node_b, w1, b1, w2, b2):
            Bx, Sx, D = x.shape
            xf = x.reshape(-1, D)
            N = xf.shape[0]
            cur = jnp.zeros((N,), jnp.int32)
            for _ in range(DEPTH):
                pw = node_w[cur]
                score = jnp.einsum('nd,nd->n', xf, pw) + node_b[cur]
                cur = 2 * cur + 1 + (score >= 0).astype(jnp.int32)
            leaf = cur - N_NODES
            sel = jax.nn.one_hot(leaf, N_LEAVES, dtype=xf.dtype)
            hidden_all = jax.nn.relu(jnp.einsum('nd,ldh->lnh', xf, w1) + b1[:, None, :])
            hidden = hidden_all * sel.T[:, :, None]
            out = jnp.einsum('lnh,lho->no', hidden, w2) + sel @ b2
            return out.reshape(Bx, Sx, D)
        q = _fff(x, q_node_w, q_node_b, q_w1, q_b1, q_w2, q_b2)
        k = _fff(x, k_node_w, k_node_b, k_w1, k_b1, k_w2, k_b2)
        v = _fff(x, v_node_w, v_node_b, v_w1, v_b1, v_w2, v_b2)
        scale = 1.0 / np.sqrt(LATENT).astype(np.float32)
        attn = jax.nn.softmax(jnp.einsum('bqd,bkd->bqk', q, k) * scale, axis=-1)
        return jnp.einsum('bqk,bkd->bqd', attn, v)
    x = x + _L0_xattn_ref(_layernorm(x, axis=-1), ctx_1024, ctx_1024, L0_xattn_w_q, L0_xattn_w_k, L0_xattn_w_v, L0_xattn_w_o)
    x = x + _L0_ffn_ref(_layernorm(x, axis=-1), L0_ffn_q_node_w, L0_ffn_q_node_b, L0_ffn_q_w1, L0_ffn_q_b1, L0_ffn_q_w2, L0_ffn_q_b2, L0_ffn_k_node_w, L0_ffn_k_node_b, L0_ffn_k_w1, L0_ffn_k_b1, L0_ffn_k_w2, L0_ffn_k_b2, L0_ffn_v_node_w, L0_ffn_v_node_b, L0_ffn_v_w1, L0_ffn_v_b1, L0_ffn_v_w2, L0_ffn_v_b2)
    return x

_drawn_inputs = setup_inputs


def setup_inputs(seed=0):
    import zlib

    import numpy as np

    out = dict(_drawn_inputs(seed))
    spreads = {'L0_ffn_q_b1': (0.0, 0.8),
     'L0_ffn_q_b2': (0.0, 0.8),
     'L0_ffn_k_b1': (0.0, 0.8),
     'L0_ffn_k_b2': (0.0, 0.8),
     'L0_ffn_v_b1': (0.0, 0.594),
     'L0_ffn_v_b2': (0.0, 0.315)}
    factors = {'L0_xattn_w_q': 8.0,
     'L0_xattn_w_k': 8.0,
     'L0_ffn_q_node_b': 7.64,
     'L0_ffn_q_w1': 2.822,
     'L0_ffn_k_node_b': 8.0,
     'L0_ffn_k_w1': 2.752,
     'L0_ffn_v_node_b': 2.772}
    for name, (base, spread) in spreads.items():
        noise = np.random.default_rng([zlib.crc32(name.encode()), seed]).standard_normal(out[name].shape)
        drawn = base * np.exp(spread * noise) if base else spread * noise
        out[name] = jnp.asarray(drawn.astype(out[name].dtype))
    for name, factor in factors.items():
        out[name] = (out[name] * factor).astype(out[name].dtype)
    return out
```

```python
from contextlib import ExitStack

import concourse.bass as bass
import numpy as np
from concourse import mybir

FP, BF, FR, I32 = mybir.dt.float32, mybir.dt.bfloat16, mybir.dt.float32r, mybir.dt.int32
ALU, ACT, AX = mybir.AluOpType, mybir.ActivationFunctionType, mybir.AxisListType

P = 128
NB, S, D = 16, 256, 256
T = S // P
C = D // P
NH = 16
DK = D // NH
HQ = 32 // DK
PARTS = 4
KS = PARTS * DK
KM = KS + 2
TREES, LEAVES, NODES, HID = 3, 16, 15, 64
TL = TREES * LEAVES
RUN = P
NTOK = NB * S
BLOCKS = (NTOK - LEAVES) // RUN + LEAVES
BLOCKS += BLOCKS % 2
ROWS = BLOCKS * RUN
WC = C * HID + D + 1
EPS = 1e-5
NEG = -3.0e38
SC = DK ** -0.5
SC2 = D ** -0.5
PAIRS = NH // 2
STACKS = 5
LAG = 3
U = 4
HORDER = [8 * c + 2 * g + par for c in range(C) for par in range(HQ) for g in range(4)]


def build(nc, x, ctxT, wqT, wkT, wvT, woT, nodeT, nodeb, leafw, out):
    ctx = ExitStack()
    scope = ExitStack()
    with ctx:
        def sb(name, shape, dt=FP, at=ctx):
            return at.enter_context(nc.sbuf_tensor(name, shape, dt))

        def sem(name):
            return ctx.enter_context(nc.semaphore(name))

        def sems(name, n=2):
            return [sem(f"{name}{i}") for i in range(n)]

        xs_dram = nc.dram_tensor("xs_dram", [TREES * ROWS, D], FP, kind="Internal").ap()
        parts_dram = [nc.dram_tensor(f"parts_dram{i}", [2, C, 2, P, S], FP, kind="Internal").ap() for i in range(2)]
        ys_dram = nc.dram_tensor("ys_dram", [TREES * ROWS, D], FP, kind="Internal").ap()
        x1_dram = nc.dram_tensor("x1_dram", [NTOK, D], FP, kind="Internal").ap()

        ident = sb("ident", [P, P])
        identb = sb("identb", [P, P], BF)
        maskb = sb("maskb", [P, P], BF)
        trib = sb("trib", [P, P], BF)
        onesb = sb("onesb", [P, P], BF)
        xn2 = sb("xn2", [P, NB, T * D])
        onehot = sb("onehot", [P, NB, T * TL], BF)
        rank = sb("rank", [P, NB, T * TREES])
        count = sb("count", [P, TL])
        place = sb("place", [P, NB * T * TREES], I32)
        blockleaf = sb("blockleaf", [P, TREES * BLOCKS], I32)
        pairs = [ctx.enter_context(nc.psum_tensor(f"banks{i}", [P, 2, 512], FP)) for i in range(4)]
        banks = [pairs[i // 2][:, i % 2, :] for i in range(8)]

        def at(name, shape, dt=FP):
            return sb(name, shape, dt, scope)

        wq, wk, wv, wo = (at(n, [P, C, D]) for n in ("wq", "wk", "wv", "wo"))
        ndT = at("ndT", [P, C, TREES * NODES])
        ndb = at("ndb", [P, T, TREES * NODES])
        zero = at("zero", [P, D])
        xt = [at(f"xt{i}", [P, T, D]) for i in range(2)]
        ct = [at(f"ct{i}", [P, C, S]) for i in range(2)]
        xr = [at(f"xr{i}", [P, T, D]) for i in range(2)]
        xn = [at(f"xn{i}", [P, T, D]) for i in range(2)]
        xnT = at("xnT", [P, C * S])
        q_hi, q_lo, k_hi, k_lo = ([at(f"{n}{i}", [P, C, S], FR) for i in range(2)]
                                  for n in ("q_hi", "q_lo", "k_hi", "k_lo"))
        q4 = [at(f"q4{i}", [KM, NH, S], FR) for i in range(2)]
        k4 = [at(f"k4{i}", [KM, NH, S], FR) for i in range(2)]
        vp = [at(f"vp{i}", [P, T, NH, 32]) for i in range(2)]
        op = at("op", [P, HQ, 32])
        pt = at("pt", [P, NH, 384])
        mneg = [at(f"mneg{i}", [P, T, NH]) for i in range(2)]
        m_hi, m_lo = at("m_hi", [NH, S], FR), at("m_lo", [NH, S], FR)
        rden = at("rden", [P, C * S])
        aT = at("aT", [P, C * S])
        x1 = [at(f"x1{i}", [P, T, D]) for i in range(2)]
        xn2s = [at(f"xn2s{i}", [P, T, D]) for i in range(2)]
        xn2T = at("xn2T", [P, C * S])
        st1, st2 = at("st1", [P, T, 6]), at("st2", [P, T, 6])
        mv1, mv2 = at("mv1", [P, T, 2]), at("mv2", [P, T, 2])
        ve1, ve2, rs1, rs2 = (at(n, [P, T]) for n in ("ve1", "ve2", "rs1", "rs2"))
        mhalf = at("mhalf", [P, T])
        sc = at("sc", [P, T, TREES * NODES])
        g2 = at("g2", [P, T * TREES, NODES, 2])
        l2, l3 = at("l2", [P, T * TREES, 4]), at("l3", [P, T * TREES, 8])
        oh = [at(f"oh{i}", [P, T * TREES * LEAVES], BF) for i in range(2)]
        rk = at("rk", [P, T, TL])
        rp = at("rp", [P, T, TL])

        scope.close()
        wl = sb("wl", [P, TL, WC])
        wb = [sb(f"wb{i}", [P, WC]) for i in range(U)]
        xb = [sb(f"xb{i}", [P, D]) for i in range(U)]
        xbT = [sb(f"xbT{i}", [P, D]) for i in range(2)]
        hT = [sb(f"hT{i}", [HID + 1, P]) for i in range(2)]
        yb = [sb(f"yb{i}", [P, D]) for i in range(U)]
        iota_t = sb("iota_t", [P, NB * T])
        iota_i = sb("iota_i", [P, NB * T + BLOCKS], I32)
        iota_b = sb("iota_b", [P, BLOCKS])
        cmp_t = sb("cmp_t", [P, TL, NB * T])
        nblk = [sb(f"nblk{i}", [P, TREES, LEAVES]) for i in range(5)]
        offs = sb("offs", [P, TREES, LEAVES])
        tmp_p = sb("tmp_p", [P, NB * T, TL])
        placef = sb("placef", [P, NB * T, TREES])
        cmp_b = sb("cmp_b", [P, TREES, BLOCKS, LEAVES])
        leaff = sb("leaff", [P, TREES * BLOCKS])
        pidx = [sb(f"pidx{i}", [P, T * TREES], I32) for i in range(2)]
        gq = [[sb(f"g{n}{i}", [P, T, D]) for n in "qkv"] for i in range(2)]
        qT, kT = ([sb(f"{n}{i}", [P, C * S]) for i in range(2)] for n in ("qT", "kT"))
        pr = [sb(f"pr{i}", [P, T, S]) for i in range(2)]
        prT = [sb(f"prT{i}", [P, T, S]) for i in range(2)]
        m2, mb2, sum2, rsum2 = ([sb(f"{n}{i}", [P, T]) for i in range(2)]
                                for n in ("m2", "mb2", "sum2", "rsum2"))
        x1r = [sb(f"x1r{i}", [P, T, D]) for i in range(2)]
        res = [sb(f"res{i}", [P, T, D]) for i in range(2)]

        consts, weights, wt_late = sem("consts"), sem("weights"), sem("wt_late")
        x_in, c_in, xr_in = sems("x_in"), sems("c_in"), sems("xr_in")
        zeroed = sem("zeroed")
        (stats1, aggr1, var1, rstd1, xn_done, xnT_ps, xnT_sb, q_ps, qh_sb, ql_sb, k_ps, kh_sb, kl_sb,
         v_ps, v_sb, s_ps, max_sb, mT_ps, mh_sb, ml_sb, st_ps, exp_sb, sel_sb, pv_ps, rden_sb, aT_sb,
         wo_ps, x1_sb, stats2, aggr2, var2, rstd2, xn2_sb, xn2_kept, xn2T_ps, xn2T_sb, node_ps, sc_sb,
         g_step, lvl2, lvl3, oh_sb, oh_kept, rank_ps, rk_sb, rp_sb, rank_kept, count_up) = (
            sem(n) for n in
            ("stats1 aggr1 var1 rstd1 xn_done xnT_ps xnT_sb q_ps qh_sb ql_sb k_ps kh_sb kl_sb "
             "v_ps v_sb s_ps max_sb mT_ps mh_sb ml_sb st_ps exp_sb sel_sb pv_ps rden_sb aT_sb "
             "wo_ps x1_sb stats2 aggr2 var2 rstd2 xn2_sb xn2_kept xn2T_ps xn2T_sb node_ps sc_sb "
             "g_step lvl2 lvl3 oh_sb oh_kept rank_ps rk_sb rp_sb rank_kept count_up").split())
        stacked = [sems("stacked_c0_"), sems("stacked_c1_")]
        unloaded = sems("unloaded")
        passed = sem("passed")
        m_row = sem("m_row")
        x1_out = sems("x1_out")
        route, iotas, placed, leaves = sem("route"), sem("iotas"), sem("placed"), sem("leaves")
        scat = sems("scat", TREES)
        (xbT_ps, xbT_sb, h_ps, h_sb, y_ps, y_sb, w_cp, hT_one) = (
            sem(n) for n in "xbT_ps xbT_sb h_ps h_sb y_ps y_sb w_cp hT_one".split())
        xb_in, y_out = sems("xb_in", U), sems("y_out", U)
        gat = sems("gat")
        (idx_cp, tq_ps, qT_sb, tk_ps, kT_sb, s2_ps, m2_sb, mb2_sb, e2_sb, rs2_sb, pT_ps, pT_sb, o_ps,
         res_sb) = (sem(n) for n in ("idx_cp tq_ps qT_sb tk_ps kT_sb s2_ps m2_sb mb2_sb e2_sb rs2_sb "
                                     "pT_ps pT_sb o_ps res_sb").split())
        x1r_in, r_out = sems("x1r_in"), sems("r_out")

        def ge(eng, semaphore, value):
            if not isinstance(value, int) or value > 0:
                eng.wait_ge(semaphore, value)

        def apart(eng):
            eng.sem_inc(passed)

        def pipeline(step, eng):
            for b in range(-2, 4):
                step(b, b // 2, b % 2)
            with eng.Fori(2, NB // 2 - 2) as i:
                for u in range(2):
                    step(i * 2 + u, i, u)
            for b in range(NB - 4, NB + 1):
                step(b, b // 2, b % 2)

        def has(b, k):
            return not isinstance(b, int) or 0 <= b + k < NB

        NCONST = 18
        S_BANKS, ST_BANKS, N_BANK, D_BANK, G6, G7 = pairs[0], pairs[1], banks[4], banks[5], banks[6], banks[7]
        block = ctx.enter_context(nc.Block())

        @block.sync
        def _(sp):
            def load_x(b, n, s):
                ge(sp, xn_done, 2 * (b - 1))
                sp.dma_start(xt[s][:], x[bass.ds(b * S, S), :].rearrange("(t p) d -> p t d", p=P)).then_inc(x_in[s], 16)

            def load_c(b, n, s):
                ge(sp, v_ps, b - 1)
                sp.dma_start(ct[s][:], ctxT[bass.ds(b * D, D), :].rearrange("(c p) k -> p c k", p=P)).then_inc(c_in[s], 16)

            def load_xr(b, n, s):
                ge(sp, x1_sb, b - 1)
                sp.dma_start(xr[s][:], x[bass.ds(b * S, S), :].rearrange("(t p) d -> p t d", p=P)).then_inc(xr_in[s], 16)

            def unload(b, n, s):
                for c in range(C):
                    ge(sp, stacked[c][s], 16 * STACKS * n)
                for m, (hi, lo, hi_sem, lo_sem) in enumerate(((q_hi, q_lo, qh_sb, ql_sb), (k_hi, k_lo, kh_sb, kl_sb))):
                    sp.wait_ge(hi_sem, b + 1)
                    sp.wait_ge(lo_sem, b + 1)
                    for r, part in enumerate((hi, lo)):
                        sp.dma_start(parts_dram[s][m, :, r].rearrange("c p k -> p c k"), part[s][:].bitcast(FP)).then_inc(unloaded[s], 16)

            def stack(b, s, c):
                hs = slice(8 * c, 8 * c + 8)

                def rows(m, r0, r1):
                    return parts_dram[s][m, c, r0:r1].rearrange("r (d h) k -> (r d) h k", h=8)

                for full, at_row, src in ((q4, 0, rows(0, 0, 2)), (q4, 2, rows(0, 1, 2)), (q4, 3, rows(0, 0, 1)),
                                          (k4, 0, rows(1, 0, 2)), (k4, 2, rows(1, 0, 2))):
                    sp.dma_start(full[s][DK * at_row:DK * at_row + src.shape[0], hs, :].bitcast(FP), src).then_inc(stacked[c][s], 16)

            def step(b, n, u):
                if has(b, 3):
                    load_x(b + 3, None, 1 - u)
                if has(b, 1):
                    load_xr(b + 1, None, 1 - u)
                if has(b, 1):
                    k = TREES * ROWS // NB
                    sp.dma_start(xs_dram[bass.ds((b + 1) * k, k), :].rearrange("(p r) d -> p r d", p=P),
                                 zero[:].unsqueeze(1).to_broadcast([P, k // P, D])).then_inc(zeroed, 16)
                if has(b, 2):
                    unload(b + 2, n + 1, u)
                    sp.wait_ge(unloaded[u], 64 * (n + 2))
                    ge(sp, st_ps, PAIRS * b + 4)
                    stack(b + 2, u, 0)
                if has(b, 3):
                    load_c(b + 3, None, 1 - u)
                if has(b, -1):
                    ge(sp, x1_sb, b)
                    sp.dma_start(x1_dram[bass.ds((b - 1) * S, S), :].rearrange("(t p) d -> p t d", p=P),
                                 x1[1 - u][:]).then_inc(x1_out[1 - u], 16)
                if has(b, 2):
                    ge(sp, st_ps, PAIRS * b + PAIRS)
                    stack(b + 2, u, 1)
                if has(b, 1):
                    ge(sp, mh_sb, b + 2)
                    ge(sp, ml_sb, b + 2)
                    sp.dma_start(q4[1 - u][KS:KS + 1, :, :].bitcast(FP), m_hi[:].bitcast(FP)).then_inc(m_row, 16)
                    sp.dma_start(q4[1 - u][KS + 1:KS + 2, :, :].bitcast(FP), m_lo[:].bitcast(FP)).then_inc(m_row, 16)

            load_x(0, 0, 0)
            load_c(0, 0, 0)
            for dst, src in ((wq, wqT), (wk, wkT), (wv, wvT), (wo, woT)):
                sp.dma_start(dst[:], src.rearrange("(c p) n -> p c n", p=P)).then_inc(weights, 16)
            sp.dma_start(ndT[:], nodeT.rearrange("(c p) n -> p c n", p=P)).then_inc(weights, 16)
            for t in range(T):
                sp.dma_start(ndb[:, t, :], nodeb.to_broadcast([P, TREES * NODES])).then_inc(weights, 16)
            sp.wait_ge(consts, NCONST)
            pipeline(step, sp)

            sp.wait_ge(count_up, NB)
            sp.wait_ge(xn2_kept, NB)
            for s in range(2):
                sp.wait_ge(x1_out[s], 16 * (NB // 2))
            for t in range(TREES):
                sp.dma_start(wl[:, t * LEAVES:(t + 1) * LEAVES, :], leafw[t]).then_inc(wt_late, 16)

            def load_block(i, u):
                g = i * U + u
                ge(sp, xbT_ps, g - U + 1)
                sp.dma_start(xb[u][:], xs_dram[bass.ds(g * RUN, RUN), :]).then_inc(xb_in[u], 16)

            for tree in range(TREES):
                sp.wait_ge(scat[tree], 16 * NB * T)
                k = BLOCKS // U
                if tree == 0:
                    for u in range(U):
                        load_block(0, u)
                with sp.Fori(tree * k + (tree == 0), (tree + 1) * k) as i:
                    for u in range(U):
                        load_block(i, u)

            def rows(ap, b):
                return ap[bass.ds(b * S, S), :].rearrange("(t p) d -> p t d", p=P)

            def final(b, n, u, first):
                if not first:
                    sp.wait_ge(res_sb, T * (b - 1))
                sp.dma_start(x1r[u][:], rows(x1_dram, b)).then_inc(x1r_in[u], 16)

            for u in range(2):
                final(u, 0, u, True)
            with sp.Fori(1, NB // 2) as i:
                for u in range(2):
                    b = i * 2 + u
                    final(b, i, u, False)
                    sp.dma_start(rows(out, b - 2), res[u][:]).then_inc(r_out[u], 16)
            for u in range(2):
                sp.wait_ge(res_sb, T * (NB - 1 + u))
                sp.dma_start(rows(out, NB - 2 + u), res[u][:]).then_inc(r_out[u], 16)
            for u in range(2):
                sp.wait_ge(r_out[u], 16 * (NB // 2))
            sp.wait_ge(zeroed, 16 * NB)

        @block.tensor
        def _(pe):
            mm = nc.tensor.matmul

            def tokens_T(b, u):
                ge(pe, xn_done, 2 * (b + 3))
                ge(pe, rk_sb, b - 1)
                ge(pe, count_up, b - 1)
                ge(pe, v_sb, b + 1)
                for t in range(T):
                    for c in range(C):
                        last = nc.tensor.transpose(G6[:, c * S + t * P:c * S + t * P + P],
                                                   xn[u][:, t, c * P:c * P + P], ident[:])
                last.then_inc(xnT_ps, 1)

            def project(ps, w, actT):
                for o in range(C):
                    for c in range(C):
                        last = mm(ps[:, o * S:o * S + S], w[:, c, o * P:o * P + P], actT(c),
                                  start=(c == 0), stop=(c == C - 1))
                return last

            def step(b, n, u):
                for j in range(PAIRS + LAG):
                    if j == 0 and has(b, 2):
                        tokens_T(b, u)
                    if j == 1 and has(b, 2):
                        pe.wait_ge(xnT_sb, b + 3)
                        ge(pe, ml_sb, b + 1)
                        ge(pe, kl_sb, b + 2)
                        project(G7, wq, lambda c: xnT[:, c * S:c * S + S]).then_inc(q_ps, 1)
                    if j == 2 and has(b, -1):
                        pe.wait_ge(aT_sb, b)
                        ge(pe, xnT_sb, b + 3 if has(b, 2) else NB)
                        ge(pe, rk_sb, b - 1)
                        ge(pe, count_up, b - 1)
                        for t in range(T):
                            for c in range(C):
                                last = mm(G6[:, t * D:t * D + D], aT[:, c * S + t * P:c * S + t * P + P],
                                          wo[:, c, :], start=(c == 0), stop=(c == C - 1))
                        last.then_inc(wo_ps, 1)
                    if j == 3 and has(b, 2):
                        pe.wait_ge(c_in[u], 16 * (n + 2))
                        pe.wait_ge(qh_sb, b + 3)
                        pe.wait_ge(ql_sb, b + 3)
                        project(G7, wk, lambda c: ct[u][:, c, :]).then_inc(k_ps, 1)
                    if j == 4 and has(b, 1):
                        pe.wait_ge(c_in[1 - u], 16 * (n + 1 + u))
                        ge(pe, x1_sb, b)
                        ge(pe, xnT_sb, b + 3 if has(b, 2) else NB)
                        for t in range(T):
                            for c in range(C):
                                last = mm(G6[:, t * D:t * D + D], ct[1 - u][:, c, t * P:t * P + P], wv[:, c, :],
                                          start=(c == 0), stop=(c == C - 1))
                        last.then_inc(v_ps, 1)
                    if j == 6 and has(b, -1):
                        pe.wait_ge(xn2_sb, 2 * b)
                        pe.wait_ge(kl_sb, b + 3 if has(b, 2) else NB)
                        for t in range(T):
                            for c in range(C):
                                last = nc.tensor.transpose(G7[:, c * S + t * P:c * S + t * P + P],
                                                           xn2s[1 - u][:, t, c * P:c * P + P], ident[:])
                        last.then_inc(xn2T_ps, 1)
                    if j == 8 and has(b, -1):
                        pe.wait_ge(xn2T_sb, b)
                        pe.wait_ge(v_sb, b + 2 if has(b, 1) else NB)
                        pe.wait_ge(x1_sb, b)
                        for t in range(T):
                            for c in range(C):
                                last = mm(G6[:, t * 64:t * 64 + TREES * NODES], xn2T[:, c * S + t * P:c * S + t * P + P],
                                          ndT[:, c, :], start=(c == 0), stop=(c == C - 1))
                        last.then_inc(node_ps, 1)
                    if j == 9 and has(b, 1):
                        pe.wait_ge(max_sb, PAIRS * (b + 2))
                        ge(pe, xn2T_sb, b)
                        ge(pe, kl_sb, b + 3 if has(b, 2) else NB)
                        for t in range(T):
                            last = nc.tensor.transpose(G7[0:NH, t * P:t * P + P], mneg[1 - u][:, t, :], ident[:])
                        last.then_inc(mT_ps, 1)
                    if j == 10 and has(b, -1):
                        pe.wait_ge(oh_sb, b)
                        o = oh[1 - u]
                        mm(G6[:, 128:128 + TL], trib[:], o[:, 0:TL], start=True, stop=True)
                        mm(G6[:, 192:192 + TL], trib[:], o[:, TL:2 * TL], start=True, stop=False)
                        mm(G6[:, 192:192 + TL], onesb[:], o[:, 0:TL], start=False, stop=True)
                        mm(G6[:, 256:256 + TL], onesb[:], o[:, 0:TL], start=True, stop=False)
                        mm(G6[:, 256:256 + TL], onesb[:], o[:, TL:2 * TL], start=False, stop=True
                           ).then_inc(rank_ps, 1)
                    if j < PAIRS and has(b, 1):
                        if j in (0, 4):
                            pe.wait_ge(stacked[j // 4][1 - u], 16 * STACKS * (n + 1 + u))
                        ge(pe, max_sb, PAIRS * (b + 1) + j)
                        for e in range(2):
                            h, ps, q, k = 2 * j + e, S_BANKS[:, e, :], q4[1 - u], k4[1 - u]
                            mm(ps[:, 0:S], q[0:KS, h, P:S], k[0:KS, h, :], start=True, stop=False)
                            mm(ps[:, P:S], identb[:], maskb[:], start=False, stop=True)
                            mm(ps[:, S:S + P], q[0:KS, h, 0:P], k[0:KS, h, 0:P], start=True, stop=False)
                            last = mm(ps[:, S:S + P], identb[:], maskb[:], start=False, stop=True)
                        last.then_inc(s_ps, 1)
                    p = j - LAG
                    if p >= 0 and has(b, 0):
                        if p == 0:
                            pe.wait_ge(m_row, 32 * (b + 1))
                        ge(pe, exp_sb, PAIRS * b + p)
                        for e in range(2):
                            h, ps, q, k = HORDER[2 * p + e], ST_BANKS[:, e, :], q4[u], k4[u]
                            mm(ps[:, 0:S], k[0:KM, h, 0:P], q[0:KM, h, :], start=True, stop=True)
                            last = mm(ps[:, S:S + P], k[0:KM, h, P:S], q[0:KM, h, P:S], start=True, stop=True)
                        last.then_inc(st_ps, 1)
                        if p % 2 and p > 1:
                            weigh(b, u, p // 2 - 1)
                if has(b, 0):
                    weigh(b, u, PAIRS // 2 - 1)

            def weigh(b, u, r):
                c, par = r // HQ, r % HQ
                pe.wait_ge(sel_sb, PAIRS * b + 2 * r + 2)
                if r == 0:
                    pe.wait_ge(v_sb, b + 1)
                    ge(pe, aT_sb, b)
                for ps, lhs in ((N_BANK, lambda kt, h: vp[u][:, kt, h, :]), (D_BANK, lambda kt, h: op[:, par, :])):
                    for kt in range(T):
                        for g in range(4):
                            t = 4 * r + g
                            last = mm(ps[32 * g:32 * g + 32, c * S + kt * P:c * S + S], lhs(kt, HORDER[t]),
                                      pt[:, t, 0:S] if kt == 0 else pt[:, t, S:S + P],
                                      start=(par == 0 and kt == 0), stop=(par == 1 and kt == 1))
                last.then_inc(pv_ps, 1)

            pe.wait_ge(consts, NCONST)
            pe.wait_ge(weights, 16 * 7)
            pipeline(step, pe)

            G = TREES * BLOCKS

            def block_in(i, u):
                g = i * U + u
                pe.wait_ge(xb_in[u], 16 * (i + 1))
                ge(pe, xbT_sb, g - 1)
                for c in range(C):
                    last = nc.tensor.transpose(banks[u % 2][:, c * P:c * P + P], xb[u][:, c * P:c * P + P], ident[:])
                last.then_inc(xbT_ps, 1)
                pe.wait_ge(xbT_sb, g + 1)
                pe.wait_ge(w_cp, g + 1)
                ge(pe, h_sb, g - 1)
                for c in range(C):
                    last = mm(banks[2 + u % 2][0:HID, 0:P], wb[u][:, c * HID:c * HID + HID],
                              xbT[u % 2][:, c * P:c * P + P], start=(c == 0), stop=(c == C - 1))
                last.then_inc(h_ps, 1)

            def block_out(i, u):
                g = i * U + u
                pe.wait_ge(h_sb, g + 1)
                ge(pe, y_sb, g - 1)
                mm(banks[4 + u % 2][:, 0:D], hT[u % 2][:], wb[u][0:HID + 1, C * HID:C * HID + D],
                   start=True, stop=True).then_inc(y_ps, 1)

            def blocks(i, more):
                for u in range(U):
                    if u < U - 1:
                        block_in(i, u + 1)
                    elif more:
                        block_in(i + 1, 0)
                    block_out(i, u)

            pe.wait_ge(hT_one, 2)
            block_in(0, 0)
            blocks(0, True)
            with pe.Fori(1, G // U - 1) as i:
                blocks(i, True)
            blocks(G // U - 1, False)

            pe.wait_ge(y_sb, G)

            def transposes(b, k, u, first):
                pe.wait_ge(gat[u], 16 * 6 * (k + 1))
                if not first:
                    pe.wait_ge(qT_sb, b)
                    pe.wait_ge(kT_sb, b)
                for ps, src, done in ((banks[0], gq[u][0], tq_ps), (banks[1], gq[u][1], tk_ps)):
                    for t in range(T):
                        for c in range(C):
                            last = nc.tensor.transpose(ps[:, c * S + t * P:c * S + t * P + P],
                                                       src[:, t, c * P:c * P + P], ident[:])
                    last.then_inc(done, 1)

            def scores(b, u, first):
                pe.wait_ge(qT_sb, b + 1)
                pe.wait_ge(kT_sb, b + 1)
                if not first:
                    pe.wait_ge(e2_sb, T * (b - 1))
                for t in range(T):
                    for c in range(C):
                        last = mm(banks[2 + u][:, t * S:t * S + S], qT[u][:, c * S + t * P:c * S + t * P + P],
                                  kT[u][:, c * S:c * S + S], start=(c == 0), stop=(c == C - 1))
                last.then_inc(s2_ps, 1)

            def probs_T(b, u, first):
                pe.wait_ge(e2_sb, T * (b + 1))
                if not first:
                    pe.wait_ge(pT_sb, b - 1)
                for qt in range(T):
                    for kt in range(T):
                        last = nc.tensor.transpose(banks[4 + u][:, kt * S + qt * P:kt * S + qt * P + P],
                                                   pr[u][:, qt, kt * P:kt * P + P], ident[:])
                last.then_inc(pT_ps, 1)

            def values(b, u, first):
                pe.wait_ge(pT_sb, b + 1)
                if not first:
                    pe.wait_ge(res_sb, T * (b - 1))
                for t in range(T):
                    for kt in range(T):
                        last = mm(banks[6 + u][:, t * D:t * D + D], prT[u][:, kt, t * P:t * P + P], gq[u][2][:, kt, :],
                                  start=(kt == 0), stop=(kt == T - 1))
                last.then_inc(o_ps, 1)

            transposes(0, 0, 0, True)
            scores(0, 0, True)
            transposes(1, 0, 1, False)
            scores(1, 1, True)
            probs_T(0, 0, True)
            values(0, 0, True)
            transposes(2, 1, 0, False)
            scores(2, 0, False)
            probs_T(1, 1, True)
            values(1, 1, True)
            with pe.Fori(1, NB // 2 - 1) as i:
                for u in range(2):
                    b = i * 2 + u
                    transposes(b + 1, i + u, 1 - u, False)
                    scores(b + 1, 1 - u, False)
                    probs_T(b, u, False)
                    values(b, u, False)
            transposes(NB - 1, NB // 2 - 1, 1, False)
            scores(NB - 1, 1, False)
            for b in (NB - 2, NB - 1):
                probs_T(b, b % 2, False)
                values(b, b % 2, False)

        @block.scalar
        def _(act):
            def step(b, n, u):
                for j in range(PAIRS + LAG):
                    p = j
                    if p == 0 and has(b, 2):
                        act.wait_ge(xnT_ps, b + 3)
                        ge(act, q_ps, b + 2)
                        nc.scalar.copy(xnT[:], G6[:]).then_inc(xnT_sb, 1)
                    if p == 1 and has(b, 2):
                        act.wait_ge(q_ps, b + 3)
                        ge(act, unloaded[u], 64 * (n + 1))
                        nc.scalar.copy(q_hi[u][:].rearrange("p c k -> p (c k)"), G7[:]).then_inc(qh_sb, 1)
                    if p == 3 and has(b, 2):
                        act.wait_ge(k_ps, b + 3)
                        nc.scalar.copy(k_hi[u][:].rearrange("p c k -> p (c k)"), G7[:]).then_inc(kh_sb, 1)
                    if p == 4 and has(b, 1):
                        act.wait_ge(v_ps, b + 2)
                        ge(act, pv_ps, 4 * b)
                        for par in range(HQ):
                            o = vp[1 - u][:].rearrange("p t (j e) c -> p (t j) e c", e=HQ)[:, :, par, DK * par:DK * par + DK]
                            i = G6[:].rearrange("p (j e c) -> p j e c", e=HQ, c=DK)[:, :, par, :]
                            last = nc.scalar.copy(o, i)
                        last.then_inc(v_sb, 1)
                    if p == 7 and has(b, -1):
                        act.wait_ge(xn2T_ps, b)
                        ge(act, node_ps, b - 1)
                        nc.scalar.copy(xn2T[:], G7[:]).then_inc(xn2T_sb, 1)
                    p = j - LAG
                    if p >= 0 and has(b, 0):
                        act.wait_ge(st_ps, PAIRS * b + p + 1)
                        if p % 2 == 0:
                            ge(act, pv_ps, 4 * (b - 1) + p // 2 + 1)
                        nc.scalar.activation(pt[:, 2 * p:2 * p + 2, :], ST_BANKS[:, :, 0:S + P], ACT.Exp,
                                             scale=SC).then_inc(exp_sb, 1)

            pipeline(step, act)

            act.wait_ge(hT_one, 2)

            def block(i, u):
                g = i * U + u
                act.wait_ge(xbT_ps, g + 1)
                ge(act, h_ps, g - 1)
                nc.scalar.copy(xbT[u % 2][:], banks[u % 2][:, 0:D]).then_inc(xbT_sb, 1)
                act.wait_ge(h_ps, g + 1)
                ge(act, y_ps, g - 1)
                nc.scalar.activation(hT[u % 2][0:HID, :], banks[2 + u % 2][0:HID, 0:P], ACT.Relu,
                                     bias=wb[u][0:HID, WC - 1:WC]).then_inc(h_sb, 1)

            def store(i, u):
                g = i * U + u
                act.wait_ge(y_sb, g + 1)
                act.dma_start(ys_dram[bass.ds(g * RUN, RUN), :], yb[u][:]).then_inc(y_out[u], 16)

            for u in range(U):
                block(0, u)
                if u >= 2:
                    store(0, u - 2)
            with act.Fori(1, TREES * BLOCKS // U) as i:
                for u in range(U):
                    block(i, u)
                    store(i - (u < 2), (u - 2) % U)
            for u in range(U - 2, U):
                store(TREES * BLOCKS // U - 1, u)

            def final(b, u, first):
                act.wait_ge(tq_ps, b + 1)
                if not first:
                    act.wait_ge(s2_ps, b - 1)
                nc.scalar.copy(qT[u][:], banks[0][:]).then_inc(qT_sb, 1)
                act.wait_ge(mb2_sb, b + 1)
                if not first:
                    act.wait_ge(pT_ps, b - 1)
                    act.wait_ge(rs2_sb, b - 1)
                for t in range(T):
                    nc.scalar.activation(pr[u][:, t, :], banks[2 + u][:, t * S:t * S + S], ACT.Exp, scale=SC2,
                                         bias=mb2[u][:, t:t + 1], accum_out=sum2[u][:, t:t + 1]).then_inc(e2_sb, 1)

            for u in range(2):
                final(u, u, True)
            with act.Fori(1, NB // 2) as i:
                for u in range(2):
                    final(i * 2 + u, u, False)

        @block.vector
        def _(v):
            def norm_in(b, n, s):
                v.wait_ge(x_in[s], 16 * (n + 1))
                for t in range(T):
                    nc.vector.bn_stats(st1[:, t, :], xt[s][:, t, :]).then_inc(stats1, 1)
                v.wait_ge(stats1, T * (b + 1))
                ge(v, rstd1, b)
                apart(v)
                for t in range(T):
                    nc.vector.bn_aggr(mv1[:, t, :], st1[:, t, :]).then_inc(aggr1, 1)

            def norm_out(b, n, s):
                v.wait_ge(rstd1, b + 1)
                ge(v, xnT_ps, b - 1)
                for t in range(T):
                    nc.vector.tensor_scalar(xn[s][:, t, :], xt[s][:, t, :], mv1[:, t, 0:1], rs1[:, t:t + 1],
                                            ALU.subtract, ALU.mult).then_inc(xn_done, 1)

            def step(b, n, u):
                for j in range(PAIRS + LAG):
                    p = j
                    if p == 0 and has(b, -1):
                        v.wait_ge(pv_ps, 4 * b)
                        nc.vector.reciprocal(rden[:], D_BANK[:]).then_inc(rden_sb, 1)
                        v.wait_ge(rden_sb, b)
                        ge(v, wo_ps, b - 1)
                        nc.vector.tensor_tensor(aT[:], N_BANK[:], rden[:], ALU.mult).then_inc(aT_sb, 1)
                    if p == 2 and has(b, 2):
                        v.wait_ge(qh_sb, b + 3)
                        nc.vector.tensor_tensor(q_lo[u][:].rearrange("p c k -> p (c k)"), G7[:],
                                                q_hi[u][:].bitcast(FP).rearrange("p c k -> p (c k)"),
                                                ALU.subtract).then_inc(ql_sb, 1)
                    if p == 3 and has(b, -1):
                        v.wait_ge(wo_ps, b)
                        v.wait_ge(xr_in[1 - u], 16 * (n + u))
                        ge(v, x1_out[1 - u], 16 * (n - 1 + u))
                        ge(v, xn2_sb, T * (b - 1))
                        nc.vector.tensor_tensor(x1[1 - u][:].rearrange("p t d -> p (t d)"), G6[:],
                                                xr[1 - u][:].rearrange("p t d -> p (t d)"), ALU.add).then_inc(x1_sb, 1)
                        v.wait_ge(x1_sb, b)
                        for t in range(T):
                            nc.vector.bn_stats(st2[:, t, :], x1[1 - u][:, t, :]).then_inc(stats2, 1)
                        v.wait_ge(stats2, T * b)
                        ge(v, rstd2, b - 1)
                        apart(v)
                        for t in range(T):
                            nc.vector.bn_aggr(mv2[:, t, :], st2[:, t, :]).then_inc(aggr2, 1)
                    if p == 4 and has(b, 2):
                        v.wait_ge(kh_sb, b + 3)
                        nc.vector.tensor_tensor(k_lo[u][:].rearrange("p c k -> p (c k)"), G7[:],
                                                k_hi[u][:].bitcast(FP).rearrange("p c k -> p (c k)"),
                                                ALU.subtract).then_inc(kl_sb, 1)
                    if p == 5 and has(b, -1):
                        v.wait_ge(rstd2, b)
                        ge(v, xn2T_ps, b - 2)
                        ge(v, xn2_kept, b - 2)
                        for t in range(T):
                            nc.vector.tensor_scalar(xn2s[1 - u][:, t, :], x1[1 - u][:, t, :], mv2[:, t, 0:1],
                                                    rs2[:, t:t + 1], ALU.subtract, ALU.mult).then_inc(xn2_sb, 1)
                    if p == 6 and has(b, 3):
                        norm_in(b + 3, *norm_slot(b, n, u))
                    if p == 8 and has(b, 3):
                        norm_out(b + 3, *norm_slot(b, n, u))
                    if p == 8 and has(b, -1):
                        tree(b, n, u)
                    if p == 9 and has(b, 1):
                        v.wait_ge(mT_ps, b + 2)
                        ge(v, m_row, 32 * (b + 1))
                        nc.vector.tensor_copy(m_hi[:], G7[0:NH, 0:S]).then_inc(mh_sb, 1)
                        v.wait_ge(mh_sb, b + 2)
                        nc.vector.tensor_tensor(m_lo[:], G7[0:NH, 0:S], m_hi[:].bitcast(FP), ALU.subtract).then_inc(ml_sb, 1)
                    if p == 10 and has(b, -1):
                        ranks(b, n, u)
                    if p < PAIRS and has(b, 1):
                        v.wait_ge(s_ps, PAIRS * (b + 1) + p + 1)
                        if p == 0:
                            ge(v, mT_ps, b)
                        for t, cols in ((1, slice(0, S)), (0, slice(S, S + P))):
                            last = nc.vector.tensor_reduce(mneg[1 - u][:, t, 2 * p:2 * p + 2], S_BANKS[:, :, cols],
                                                           axis=AX.X, op=ALU.max, negate=True)
                        last.then_inc(max_sb, 1)

            def norm_slot(b, n, u):
                return n + 1 + u, 1 - u

            def tree(b, n, u):
                v.wait_ge(node_ps, b)
                nc.vector.tensor_tensor(sc[:], G6[:, 0:128].rearrange("p (t m) -> p t m", t=T)[:, :, 0:TREES * NODES],
                                        ndb[:], ALU.add).then_inc(sc_sb, 1)
                v.wait_ge(sc_sb, b)
                scr = sc[:].rearrange("p t (r m) -> p (t r) m", m=NODES)
                nc.vector.tensor_scalar(g2[:, :, :, 1], scr, 0.0, None, ALU.is_ge).then_inc(g_step, 1)
                nc.vector.tensor_scalar(g2[:, :, :, 0], scr, 0.0, None, ALU.is_lt).then_inc(g_step, 1)
                v.wait_ge(g_step, 2 * b)
                R = T * TREES
                src = g2[:, :, 0, :]
                for lvl, (dst, done) in enumerate(((l2[:], lvl2), (l3[:], lvl3),
                                                   (oh[1 - u][:].rearrange("p (r l) -> p r l", l=LEAVES), oh_sb))):
                    m = 2 << lvl
                    if done is oh_sb:
                        ge(v, oh_kept, b - 2)
                        ge(v, rank_ps, b - 2)
                        ge(v, rp_sb, b - 2)
                    nc.vector.tensor_tensor(dst.rearrange("p r (m e) -> p r m e", e=2),
                                            src.unsqueeze(3).to_broadcast([P, R, m, 2]),
                                            g2[:, :, m - 1:2 * m - 1, :], ALU.mult).then_inc(done, 1)
                    v.wait_ge(done, b)
                    src = dst

            def ranks(b, n, u):
                v.wait_ge(rank_ps, b)
                ge(v, count_up, b - 1)
                nc.vector.tensor_tensor(rk[:], G6[:, 128:256].rearrange("p (t m) -> p t m", t=T)[:, :, 0:TL],
                                        count[:].unsqueeze(1).to_broadcast([P, T, TL]), ALU.add).then_inc(rk_sb, 1)
                v.wait_ge(rk_sb, b)
                nc.vector.tensor_tensor(rp[:].rearrange("p t m -> p (t m)"), rk[:].rearrange("p t m -> p (t m)"),
                                        oh[1 - u][:], ALU.mult).then_inc(rp_sb, 1)
                nc.vector.tensor_tensor(count[:], count[:], G6[:, 256:256 + TL], ALU.add).then_inc(count_up, 1)
                v.wait_ge(rp_sb, b)
                nc.vector.tensor_reduce(rank[:, bass.ds(b - 1, 1), :], rp[:].rearrange("p t (r l) -> p (t r) l", l=LEAVES),
                                        axis=AX.X, op=ALU.add).then_inc(rank_kept, 1)
                nc.vector.tensor_copy(onehot[:, bass.ds(b - 1, 1), :], oh[1 - u][:]).then_inc(oh_kept, 1)

            for s in range(2):
                nc.vector.memset(k4[s][KS:KM, :, :].bitcast(FP), 1.0).then_inc(consts, 1)
            v.wait_ge(consts, NCONST)
            v.wait_ge(weights, 16 * 7)
            for b0 in range(1):
                norm_in(b0, 0, b0)
                norm_out(b0, 0, b0)
            pipeline(step, v)

            steps = [0]

            def done(ins):
                steps[0] += 1
                ins.then_inc(route, 1)
                v.wait_ge(route, steps[0])

            v.wait_ge(count_up, NB)
            v.wait_ge(rank_kept, NB)
            v.wait_ge(oh_kept, NB)
            v.wait_ge(iotas, 2)
            done(nc.vector.tensor_copy(iota_t[:], iota_i[:, 0:NB * T]))
            done(nc.vector.tensor_copy(iota_b[:], iota_i[:, NB * T:]))
            done(nc.vector.tensor_tensor(cmp_t[:], count[:].unsqueeze(2).to_broadcast([P, TL, NB * T]),
                                         iota_t[:].unsqueeze(1).to_broadcast([P, TL, NB * T]), ALU.is_gt))
            done(nc.vector.tensor_reduce(nblk[0][:].rearrange("p r l -> p (r l)"), cmp_t[:], axis=AX.X, op=ALU.add))
            for k in range(4):
                w, a, o = 1 << k, nblk[k], nblk[k + 1]
                done(nc.vector.tensor_tensor(o[:, :, w:], a[:, :, w:], a[:, :, 0:LEAVES - w], ALU.add))
                done(nc.vector.tensor_copy(o[:, :, 0:w], a[:, :, 0:w]))
            done(nc.vector.tensor_tensor(offs[:], nblk[4][:], nblk[0][:], ALU.subtract))
            for r in range(TREES):
                done(nc.vector.tensor_scalar(nblk[1][:, r, :], offs[:, r, :], float(RUN), float(r * ROWS), ALU.mult, ALU.add))
            done(nc.vector.tensor_tensor(tmp_p[:], onehot[:].rearrange("p b (t m) -> p (b t) m", t=T),
                                         nblk[1][:].rearrange("p r l -> p (r l)").unsqueeze(1).to_broadcast([P, NB * T, TL]),
                                         ALU.mult))
            done(nc.vector.tensor_reduce(placef[:].rearrange("p t r -> p (t r)"),
                                         tmp_p[:].rearrange("p t (r l) -> p (t r) l", l=LEAVES), axis=AX.X, op=ALU.add))
            nc.vector.tensor_tensor(place[:], placef[:].rearrange("p t r -> p (t r)"),
                                    rank[:].rearrange("p b m -> p (b m)"), ALU.add).then_inc(placed, 1)
            for r in range(TREES):
                last = nc.vector.tensor_tensor(cmp_b[:, r], iota_b[:].unsqueeze(2).to_broadcast([P, BLOCKS, LEAVES]),
                                               nblk[4][:, r, :].unsqueeze(1).to_broadcast([P, BLOCKS, LEAVES]), ALU.is_ge)
                done(last)
            done(nc.vector.tensor_reduce(leaff[:], cmp_b[:].rearrange("p r b l -> p (r b) l"), axis=AX.X, op=ALU.add))
            for r in range(TREES):
                bs = slice(r * BLOCKS, (r + 1) * BLOCKS)
                last = nc.vector.tensor_scalar(blockleaf[:, bs], leaff[:, bs], float(LEAVES - 1), float(r * LEAVES),
                                               ALU.min, ALU.add)
            last.then_inc(leaves, 1)

            for u in range(2):
                nc.vector.memset(hT[u][HID:HID + 1, :], 1.0).then_inc(hT_one, 1)
            v.wait_ge(wt_late, 16 * TREES)
            v.wait_ge(leaves, 1)

            def take_weights(i, u):
                g = i * U + u
                leaf = v.value_load(blockleaf[0:1, bass.ds(g, 1)], min_val=0, max_val=TL - 1)
                ge(v, y_ps, g - U + 1)
                nc.vector.tensor_copy(wb[u][:], wl[:, bass.ds(leaf, 1), :].rearrange("p o n -> p (o n)")).then_inc(w_cp, 1)

            def copy_y(i, u):
                v.wait_ge(y_ps, i * U + u + 1)
                ge(v, y_out[u], 16 * i)
                nc.vector.tensor_copy(yb[u][:], banks[4 + u % 2][:, 0:D]).then_inc(y_sb, 1)

            for u in range(U):
                take_weights(0, u)
            k = TREES * BLOCKS // U
            for u in range(U):
                copy_y(0, u)
                take_weights(1, u)
            with v.Fori(1, k - 1) as i:
                for u in range(U):
                    copy_y(i, u)
                    take_weights(i + 1, u)
            for u in range(U):
                copy_y(k - 1, u)

            def kcopy(b, u, first):
                v.wait_ge(tk_ps, b + 1)
                if not first:
                    v.wait_ge(s2_ps, b - 1)
                nc.vector.tensor_copy(kT[u][:], banks[1][:]).then_inc(kT_sb, 1)

            def maxima(b, u, first):
                v.wait_ge(s2_ps, b + 1)
                nc.vector.tensor_reduce(m2[u][:], banks[2 + u][:].rearrange("p (t k) -> p t k", t=T), axis=AX.X,
                                        op=ALU.max, negate=True).then_inc(m2_sb, 1)
                v.wait_ge(m2_sb, b + 1)
                if not first:
                    v.wait_ge(e2_sb, T * (b - 1))
                nc.vector.tensor_scalar(mb2[u][:], m2[u][:], SC2, None, ALU.mult).then_inc(mb2_sb, 1)

            def finish(b, k, u, first):
                v.wait_ge(pT_ps, b + 1)
                if not first:
                    v.wait_ge(o_ps, b - 1)
                nc.vector.tensor_copy(prT[u][:].rearrange("p t k -> p (t k)"), banks[4 + u][:]).then_inc(pT_sb, 1)
                nc.vector.reciprocal(rsum2[u][:], sum2[u][:]).then_inc(rs2_sb, 1)
                v.wait_ge(rs2_sb, b + 1)
                v.wait_ge(o_ps, b + 1)
                v.wait_ge(x1r_in[u], 16 * (k + 1))
                if not first:
                    v.wait_ge(r_out[u], 16 * k)
                for t in range(T):
                    nc.vector.scalar_tensor_tensor(res[u][:, t, :], banks[6 + u][:, t * D:t * D + D],
                                                   rsum2[u][:, t:t + 1], x1r[u][:, t, :],
                                                   ALU.mult, ALU.add).then_inc(res_sb, 1)

            kcopy(0, 0, True)
            maxima(0, 0, True)
            kcopy(1, 1, True)
            maxima(1, 1, True)
            finish(0, 0, 0, True)
            kcopy(2, 0, False)
            maxima(2, 0, False)
            finish(1, 0, 1, True)
            with v.Fori(1, NB // 2 - 1) as i:
                for u in range(2):
                    b = i * 2 + u
                    kcopy(b + 1, 1 - u, False)
                    maxima(b + 1, 1 - u, False)
                    finish(b, i, u, False)
            kcopy(NB - 1, 1, False)
            maxima(NB - 1, 1, False)
            for u in range(2):
                finish(NB - 2 + u, NB // 2 - 1, u, False)

        @block.gpsimd
        def _(gp):
            pool = nc.gpsimd
            for tile, value in ((ident, 0.0), (maskb, 0.0), (trib, 1.0), (onesb, 1.0), (mhalf, -0.5), (zero, 0.0),
                                (count, 0.0), (op, 0.0), (vp[0], 0.0), (vp[1], 0.0)):
                pool.memset(tile[:], value).then_inc(consts, 1)
            gp.wait_ge(consts, 12)
            pool.affine_select(out=ident[:], in_=ident[:], compare_op=ALU.not_equal, fill=1.0, base=0,
                               pattern=[[-1, P]], channel_multiplier=1).then_inc(consts, 1)
            pool.affine_select(out=maskb[:], in_=maskb[:], compare_op=ALU.is_ge, fill=NEG, base=0,
                               pattern=[[-1, P]], channel_multiplier=1).then_inc(consts, 1)
            pool.affine_select(out=trib[:], in_=trib[:], compare_op=ALU.is_gt, fill=0.0, base=0,
                               pattern=[[1, P]], channel_multiplier=-1).then_inc(consts, 1)
            for par in range(HQ):
                pool.memset(op[:, par, DK * par:DK * par + DK], 1.0).then_inc(consts, 1)
            gp.wait_ge(consts, 17)
            pool.tensor_copy(identb[:], ident[:]).then_inc(consts, 1)
            gp.wait_ge(consts, NCONST)

            def rsqrt(b, aggr, mv, ve, var_sem, rs, rstd_sem, prev_read):
                gp.wait_ge(aggr, T * (b + 1))
                ge(gp, *prev_read)
                apart(gp)
                pool.tensor_scalar(ve[:], mv[:, :, 1], EPS, None, ALU.add).then_inc(var_sem, 1)
                gp.wait_ge(var_sem, b + 1)
                pool.tensor_tensor(rs[:], ve[:], mhalf[:], ALU.pow).then_inc(rstd_sem, 1)

            def step(b, n, u):
                for j in range(PAIRS + LAG):
                    p = j
                    if p == 4 and has(b, -1):
                        rsqrt(b - 1, aggr2, mv2, ve2, var2, rs2, rstd2, (xn2_sb, T * (b - 1)))
                    if p == 7 and has(b, 3):
                        rsqrt(b + 3, aggr1, mv1, ve1, var1, rs1, rstd1, (xn_done, T * (b + 3)))
                    if p == 9 and has(b, -1):
                        gp.wait_ge(xn2_sb, T * b)
                        pool.tensor_copy(xn2[:, bass.ds(b - 1, 1), :],
                                         xn2s[1 - u][:].rearrange("p t d -> p (t d)")).then_inc(xn2_kept, 1)
                    p = j - LAG
                    if p >= 0 and has(b, 0):
                        gp.wait_ge(exp_sb, PAIRS * b + p + 1)
                        apart(gp)
                        for cols in (slice(0, P), slice(S, S + P)):
                            dg = pt[:, 2 * p:2 * p + 2, cols]
                            last = pool.affine_select(out=dg, in_=dg, compare_op=ALU.is_ge, fill=0.0, base=0,
                                                      pattern=[[0, 2], [1, P]], channel_multiplier=-1)
                        last.then_inc(sel_sb, 1)

            rsqrt(0, aggr1, mv1, ve1, var1, rs1, rstd1, (xn_done, 0))
            pipeline(step, gp)

            gp.wait_ge(count_up, NB)
            for s in range(2):
                gp.wait_ge(x1_out[s], 16 * (NB // 2))
            pool.iota(iota_i[:, 0:NB * T], pattern=[[P, NB * T]], base=0, channel_multiplier=0).then_inc(iotas, 1)
            pool.iota(iota_i[:, NB * T:], pattern=[[1, BLOCKS]], base=0, channel_multiplier=0).then_inc(iotas, 1)
            gp.wait_ge(placed, 1)
            gp.wait_ge(zeroed, 16 * NB)
            gp.wait_ge(xn2_kept, NB)

            def scatter(tree):
                for t in range(NB * T):
                    k = t * TREES + tree
                    gp.indirect_dma_start(xs_dram, bass.IndirectOffsetOnAxis(ap=place[:, k:k + 1], axis=0),
                                          xn2[:, t // T, (t % T) * D:(t % T) * D + D], None).then_inc(scat[tree], 16)

            for tree in range(TREES):
                scatter(tree)

            for s in range(U):
                gp.wait_ge(y_out[s], 16 * TREES * BLOCKS // U)

            def gather(b, k, u, first):
                if not first:
                    gp.wait_ge(o_ps, b - 1)
                    gp.wait_ge(gat[u], 16 * 6 * k)
                pool.tensor_copy(pidx[u][:], place[:, bass.ds(b * T * TREES, T * TREES)]).then_inc(idx_cp, 1)
                gp.wait_ge(idx_cp, b + 1)
                apart(gp)
                for tree in range(TREES):
                    for t in range(T):
                        m = t * TREES + tree
                        gp.indirect_dma_start(gq[u][tree][:, t, :], None, ys_dram,
                                              bass.IndirectOffsetOnAxis(ap=pidx[u][:, m:m + 1], axis=0)
                                              ).then_inc(gat[u], 16)

            for u in range(2):
                gather(u, 0, u, True)
            with gp.Fori(1, NB // 2) as i:
                for u in range(2):
                    gather(i * 2 + u, i, u, False)


def kernel(**a):
    import concourse.bacc as bacc
    from concourse.bass_utils import run_bass_kernel_spmd as run

    a = {k: np.asarray(v) for k, v in a.items()}
    n = {k: a[f"L0_xattn_{k}"] for k in ("w_q", "w_k", "w_v", "w_o")}
    f = {k: np.stack([a[f"L0_ffn_{t}_{k}"] for t in "qkv"]) for k in ("node_w", "node_b", "w1", "b1", "w2", "b2")}
    leafw = np.zeros((TREES, P, LEAVES, WC), np.float32)
    for c in range(C):
        leafw[:, :, :, c * HID:(c + 1) * HID] = f["w1"][:, :, c * P:(c + 1) * P, :].transpose(0, 2, 1, 3)
    leafw[:, 0:HID, :, C * HID:C * HID + D] = f["w2"].transpose(0, 2, 1, 3)
    leafw[:, HID, :, C * HID:C * HID + D] = f["b2"]
    leafw[:, 0:HID, :, WC - 1] = f["b1"].transpose(0, 2, 1)

    def by_dim(w):
        return w.reshape(D, C, NH // C, DK).transpose(0, 1, 3, 2).reshape(D, D)

    arrays = {
        "x": a["x"].reshape(NTOK, D),
        "ctxT": a["ctx_1024"].transpose(0, 2, 1).reshape(NB * D, S),
        "wqT": by_dim(n["w_q"].T), "wkT": by_dim(n["w_k"].T), "wvT": n["w_v"].T, "woT": n["w_o"].T,
        "nodeT": f["node_w"].reshape(TREES * NODES, D).T,
        "nodeb": f["node_b"].reshape(1, TREES * NODES),
        "leafw": leafw,
    }
    arrays = {k: np.ascontiguousarray(v) for k, v in arrays.items()}
    nc = bacc.Bacc("TRN2", target_bir_lowering=False, num_devices=1)
    args = {k: nc.dram_tensor(k, v.shape, mybir.dt.from_np(v.dtype), kind="ExternalInput").ap()
            for k, v in arrays.items()}
    out = nc.dram_tensor("out", (NTOK, D), FP, kind="ExternalOutput").ap()
    build(nc, **args, out=out)
    r = run(nc, [arrays], core_ids=[0])
    return r.results[0]["out"].reshape(NB, S, D)
```

```python
from contextlib import ExitStack

import concourse.bass as bass
import numpy as np
from concourse import mybir

FP, BF, FR, I32 = mybir.dt.float32, mybir.dt.bfloat16, mybir.dt.float32r, mybir.dt.int32
ALU, ACT, AX = mybir.AluOpType, mybir.ActivationFunctionType, mybir.AxisListType

P = 128
NB, S, D = 16, 256, 256
T = S // P
C = D // P
NH = 16
DK = D // NH
HQ = 32 // DK
PARTS = 4
KS = PARTS * DK
KM = KS + 2
TREES, LEAVES, NODES, HID = 3, 16, 15, 64
TL = TREES * LEAVES
RUN = P
NTOK = NB * S
BLOCKS = (NTOK - LEAVES) // RUN + LEAVES
BLOCKS += BLOCKS % 2
ROWS = BLOCKS * RUN
WC = C * HID + D + 1
EPS = 1e-5
NEG = -3.0e38
SC = DK ** -0.5
SC2 = D ** -0.5
PAIRS = NH // 2
STACKS = 5
LAG = 3
U = 4
HORDER = [8 * c + 2 * g + par for c in range(C) for par in range(HQ) for g in range(4)]


def build(nc, x, ctxT, wqT, wkT, wvT, woT, nodeT, nodeb, leafw, out):
    ctx = ExitStack()
    scope = ExitStack()
    with ctx:
        def sb(name, shape, dt=FP, at=ctx):
            return at.enter_context(nc.sbuf_tensor(name, shape, dt))

        def sem(name):
            return ctx.enter_context(nc.semaphore(name))

        def sems(name, n=2):
            return [sem(f"{name}{i}") for i in range(n)]

        xs_dram = [nc.dram_tensor(f"xs_dram{t}", [ROWS, D], FP, kind="Internal").ap() for t in range(TREES)]
        parts_dram = [nc.dram_tensor(f"parts_dram{i}", [2, C, 2, P, S], FP, kind="Internal").ap() for i in range(2)]
        ys_dram = [nc.dram_tensor(f"ys_dram{t}", [ROWS, D], FP, kind="Internal").ap() for t in range(TREES)]
        x1_dram = nc.dram_tensor("x1_dram", [NTOK, D], FP, kind="Internal").ap()

        ident = sb("ident", [P, P])
        identb = sb("identb", [P, P], BF)
        maskb = sb("maskb", [P, P], BF)
        trib = sb("trib", [P, P], BF)
        onesb = sb("onesb", [P, P], BF)
        xn2 = sb("xn2", [P, NB, T * D])
        onehot = sb("onehot", [P, NB, T * TL], BF)
        rank = sb("rank", [P, NB, T * TREES])
        count = sb("count", [P, TL])
        place = sb("place", [P, NB * T * TREES], I32)
        blockleaf = sb("blockleaf", [P, TREES * BLOCKS], I32)
        pairs = [ctx.enter_context(nc.psum_tensor(f"banks{i}", [P, 2, 512], FP)) for i in range(4)]
        banks = [pairs[i // 2][:, i % 2, :] for i in range(8)]

        def at(name, shape, dt=FP):
            return sb(name, shape, dt, scope)

        wq, wk, wv, wo = (at(n, [P, C, D]) for n in ("wq", "wk", "wv", "wo"))
        ndT = at("ndT", [P, C, TREES * NODES])
        ndb = at("ndb", [P, T, TREES * NODES])
        zero = at("zero", [P, D])
        xt = [at(f"xt{i}", [P, T, D]) for i in range(2)]
        ct = [at(f"ct{i}", [P, C, S]) for i in range(2)]
        xr = [at(f"xr{i}", [P, T, D]) for i in range(2)]
        xn = [at(f"xn{i}", [P, T, D]) for i in range(2)]
        xnT = at("xnT", [P, C * S])
        q_hi, q_lo, k_hi, k_lo = ([at(f"{n}{i}", [P, C, S], FR) for i in range(2)]
                                  for n in ("q_hi", "q_lo", "k_hi", "k_lo"))
        q4 = [at(f"q4{i}", [KM, NH, S], FR) for i in range(2)]
        k4 = [at(f"k4{i}", [KM, NH, S], FR) for i in range(2)]
        vp = [at(f"vp{i}", [P, T, NH, 32]) for i in range(2)]
        op = at("op", [P, HQ, 32])
        pt = at("pt", [P, NH, 384])
        mneg = [at(f"mneg{i}", [P, T, NH]) for i in range(2)]
        m_hi, m_lo = at("m_hi", [NH, S], FR), at("m_lo", [NH, S], FR)
        rden = at("rden", [P, C * S])
        aT = at("aT", [P, C * S])
        x1 = [at(f"x1{i}", [P, T, D]) for i in range(2)]
        xn2s = [at(f"xn2s{i}", [P, T, D]) for i in range(2)]
        xn2T = at("xn2T", [P, C * S])
        st1, st2 = at("st1", [P, T, 6]), at("st2", [P, T, 6])
        mv1, mv2 = at("mv1", [P, T, 2]), at("mv2", [P, T, 2])
        ve1, ve2, rs1, rs2 = (at(n, [P, T]) for n in ("ve1", "ve2", "rs1", "rs2"))
        mhalf = at("mhalf", [P, T])
        sc = at("sc", [P, T, TREES * NODES])
        g2 = at("g2", [P, T * TREES, NODES, 2])
        l2, l3 = at("l2", [P, T * TREES, 4]), at("l3", [P, T * TREES, 8])
        oh = [at(f"oh{i}", [P, T * TREES * LEAVES], BF) for i in range(2)]
        rk = at("rk", [P, T, TL])
        rp = at("rp", [P, T, TL])

        scope.close()
        wb = [sb(f"wb{i}", [P, WC]) for i in range(U)]
        xb = [sb(f"xb{i}", [P, D]) for i in range(U)]
        xbT = [sb(f"xbT{i}", [P, D]) for i in range(2)]
        hT = [sb(f"hT{i}", [HID + 1, P]) for i in range(2)]
        yb = [sb(f"yb{i}", [P, D]) for i in range(U)]
        iota_i = sb("iota_i", [P, NB * T + BLOCKS], I32)
        nblk = [sb(f"nblk{i}", [P, TREES, LEAVES]) for i in range(5)]
        q_all = sb("q_all", [P, NB, T * D])
        ffn = ExitStack()
        wl = sb("wl", [P, TL, WC], FP, ffn)
        iota_t = sb("iota_t", [P, NB * T], FP, ffn)
        iota_b = sb("iota_b", [P, BLOCKS], FP, ffn)
        cmp_t = sb("cmp_t", [P, TL, NB * T], FP, ffn)
        offs = sb("offs", [P, TREES, LEAVES], FP, ffn)
        tmp_p = sb("tmp_p", [P, NB * T, TL], FP, ffn)
        placef = sb("placef", [P, NB * T, TREES], FP, ffn)
        cmp_b = sb("cmp_b", [P, TREES, BLOCKS, LEAVES], FP, ffn)
        leaff = sb("leaff", [P, TREES * BLOCKS], FP, ffn)
        ffn.close()

        pidx = [sb(f"pidx{i}", [P, T * TREES], I32) for i in range(U)]
        k_all = xn2
        qr, kr, vr = ([sb(f"{n}{i}", [P, T, D]) for i in range(U)] for n in ("qr", "kr", "vr"))
        qT, kT = ([sb(f"{n}{i}", [P, C * S]) for i in range(2)] for n in ("qT", "kT"))
        pr = [sb(f"pr{i}", [P, T, S]) for i in range(2)]
        prT = [sb(f"prT{i}", [P, T, S]) for i in range(2)]
        m2, mb2, sum2, rsum2 = ([sb(f"{n}{i}", [P, T]) for i in range(2)]
                                for n in ("m2", "mb2", "sum2", "rsum2"))
        x1r = [sb(f"x1r{i}", [P, T, D]) for i in range(U)]
        res = [sb(f"res{i}", [P, T, D]) for i in range(U)]

        consts, weights, wt_late = sem("consts"), sem("weights"), sem("wt_late")
        x_in, c_in, xr_in = sems("x_in"), sems("c_in"), sems("xr_in")
        zeroed = sem("zeroed")
        (stats1, aggr1, var1, rstd1, xn_done, xnT_ps, xnT_sb, q_ps, qh_sb, ql_sb, k_ps, kh_sb, kl_sb,
         v_ps, v_sb, s_ps, max_sb, mT_ps, mh_sb, ml_sb, st_ps, exp_sb, sel_sb, pv_ps, rden_sb, aT_sb,
         wo_ps, x1_sb, stats2, aggr2, var2, rstd2, xn2_sb, xn2_kept, xn2T_ps, xn2T_sb, node_ps, sc_sb,
         g_step, lvl2, lvl3, oh_sb, oh_kept, rank_ps, rk_sb, rp_sb, rank_kept, count_up) = (
            sem(n) for n in
            ("stats1 aggr1 var1 rstd1 xn_done xnT_ps xnT_sb q_ps qh_sb ql_sb k_ps kh_sb kl_sb "
             "v_ps v_sb s_ps max_sb mT_ps mh_sb ml_sb st_ps exp_sb sel_sb pv_ps rden_sb aT_sb "
             "wo_ps x1_sb stats2 aggr2 var2 rstd2 xn2_sb xn2_kept xn2T_ps xn2T_sb node_ps sc_sb "
             "g_step lvl2 lvl3 oh_sb oh_kept rank_ps rk_sb rp_sb rank_kept count_up").split())
        stacked = [sems("stacked_c0_"), sems("stacked_c1_")]
        unloaded = sems("unloaded")
        passed = sem("passed")
        m_row = sem("m_row")
        x1_out = sems("x1_out")
        route, iotas, placed, leaves = sem("route"), sem("iotas"), sem("placed"), sem("leaves")
        scat = sems("scat", TREES)
        (xbT_ps, xbT_sb, h_ps, h_sb, y_ps, y_sb, w_cp, hT_one) = (
            sem(n) for n in "xbT_ps xbT_sb h_ps h_sb y_ps y_sb w_cp hT_one".split())
        xb_in, y_out = sems("xb_in", U), sems("y_out", U)
        q_in, k_in = sem("q_in"), sem("k_in")
        qk_in, v_in = sems("qk_in", U), sems("v_in", U)
        (idx_cp, tq_ps, qT_sb, tk_ps, kT_sb, s2_ps, m2_sb, mb2_sb, e2_sb, rs2_sb, pT_ps, pT_sb, o_ps,
         res_sb) = (sem(n) for n in ("idx_cp tq_ps qT_sb tk_ps kT_sb s2_ps m2_sb mb2_sb e2_sb rs2_sb "
                                     "pT_ps pT_sb o_ps res_sb").split())
        x1r_in, r_out = sems("x1r_in", U), sems("r_out", U)

        def ge(eng, semaphore, value):
            if not isinstance(value, int) or value > 0:
                eng.wait_ge(semaphore, value)

        def apart(eng):
            eng.sem_inc(passed)

        def pipeline(step, eng):
            for b in range(-2, 4):
                step(b, b // 2, b % 2)
            with eng.Fori(2, NB // 2 - 2) as i:
                for u in range(2):
                    step(i * 2 + u, i, u)
            for b in range(NB - 4, NB + 1):
                step(b, b // 2, b % 2)

        def has(b, k):
            return not isinstance(b, int) or 0 <= b + k < NB

        NCONST = 18
        S_BANKS, ST_BANKS, N_BANK, D_BANK, G6, G7 = pairs[0], pairs[1], banks[4], banks[5], banks[6], banks[7]
        block = ctx.enter_context(nc.Block())

        @block.sync
        def _(sp):
            def load_x(b, n, s):
                ge(sp, xn_done, 2 * (b - 1))
                sp.dma_start(xt[s][:], x[bass.ds(b * S, S), :].rearrange("(t p) d -> p t d", p=P)).then_inc(x_in[s], 16)

            def load_c(b, n, s):
                ge(sp, v_ps, b - 1)
                sp.dma_start(ct[s][:], ctxT[bass.ds(b * D, D), :].rearrange("(c p) k -> p c k", p=P)).then_inc(c_in[s], 16)

            def load_xr(b, n, s):
                ge(sp, x1_sb, b - 1)
                sp.dma_start(xr[s][:], x[bass.ds(b * S, S), :].rearrange("(t p) d -> p t d", p=P)).then_inc(xr_in[s], 16)

            def unload(b, n, s):
                for c in range(C):
                    ge(sp, stacked[c][s], 16 * STACKS * n)
                for m, (hi, lo, hi_sem, lo_sem) in enumerate(((q_hi, q_lo, qh_sb, ql_sb), (k_hi, k_lo, kh_sb, kl_sb))):
                    sp.wait_ge(hi_sem, b + 1)
                    sp.wait_ge(lo_sem, b + 1)
                    for r, part in enumerate((hi, lo)):
                        sp.dma_start(parts_dram[s][m, :, r].rearrange("c p k -> p c k"), part[s][:].bitcast(FP)).then_inc(unloaded[s], 16)

            def stack(b, s, c):
                hs = slice(8 * c, 8 * c + 8)

                def rows(m, r0, r1):
                    return parts_dram[s][m, c, r0:r1].rearrange("r (d h) k -> (r d) h k", h=8)

                for full, at_row, src in ((q4, 0, rows(0, 0, 2)), (q4, 2, rows(0, 1, 2)), (q4, 3, rows(0, 0, 1)),
                                          (k4, 0, rows(1, 0, 2)), (k4, 2, rows(1, 0, 2))):
                    sp.dma_start(full[s][DK * at_row:DK * at_row + src.shape[0], hs, :].bitcast(FP), src).then_inc(stacked[c][s], 16)

            def step(b, n, u):
                if has(b, 3):
                    load_x(b + 3, None, 1 - u)
                if has(b, 1):
                    load_xr(b + 1, None, 1 - u)
                if has(b, 1):
                    k = ROWS // NB
                    for tree in range(TREES):
                        sp.dma_start(xs_dram[tree][bass.ds((b + 1) * k, k), :].rearrange("(p r) d -> p r d", p=P),
                                     zero[:].unsqueeze(1).to_broadcast([P, k // P, D])).then_inc(zeroed, 16)
                if has(b, 2):
                    unload(b + 2, n + 1, u)
                    sp.wait_ge(unloaded[u], 64 * (n + 2))
                    ge(sp, st_ps, PAIRS * b + 4)
                    stack(b + 2, u, 0)
                if has(b, 3):
                    load_c(b + 3, None, 1 - u)
                if has(b, -1):
                    ge(sp, x1_sb, b)
                    sp.dma_start(x1_dram[bass.ds((b - 1) * S, S), :].rearrange("(t p) d -> p t d", p=P),
                                 x1[1 - u][:]).then_inc(x1_out[1 - u], 16)
                if has(b, 2):
                    ge(sp, st_ps, PAIRS * b + PAIRS)
                    stack(b + 2, u, 1)
                if has(b, 1):
                    ge(sp, mh_sb, b + 2)
                    ge(sp, ml_sb, b + 2)
                    sp.dma_start(q4[1 - u][KS:KS + 1, :, :].bitcast(FP), m_hi[:].bitcast(FP)).then_inc(m_row, 16)
                    sp.dma_start(q4[1 - u][KS + 1:KS + 2, :, :].bitcast(FP), m_lo[:].bitcast(FP)).then_inc(m_row, 16)

            load_x(0, 0, 0)
            load_c(0, 0, 0)
            for dst, src in ((wq, wqT), (wk, wkT), (wv, wvT), (wo, woT)):
                sp.dma_start(dst[:], src.rearrange("(c p) n -> p c n", p=P)).then_inc(weights, 16)
            sp.dma_start(ndT[:], nodeT.rearrange("(c p) n -> p c n", p=P)).then_inc(weights, 16)
            for t in range(T):
                sp.dma_start(ndb[:, t, :], nodeb.to_broadcast([P, TREES * NODES])).then_inc(weights, 16)
            sp.wait_ge(consts, NCONST)
            pipeline(step, sp)

            sp.wait_ge(count_up, NB)
            sp.wait_ge(xn2_kept, NB)
            for s in range(2):
                sp.wait_ge(x1_out[s], 16 * (NB // 2))
            for t in range(TREES):
                sp.dma_start(wl[:, t * LEAVES:(t + 1) * LEAVES, :], leafw[t]).then_inc(wt_late, 16)

            def load_block(tree, i, u):
                g = i * U + u
                ge(sp, xbT_ps, g - U + 1)
                sp.dma_start(xb[u][:], xs_dram[tree][bass.ds((g - tree * BLOCKS) * RUN, RUN), :]).then_inc(xb_in[u], 16)

            for tree in range(TREES):
                sp.wait_ge(scat[tree], 16 * NB * T)
                k = BLOCKS // U
                if tree == 0:
                    for u in range(U):
                        load_block(0, 0, u)
                with sp.Fori(tree * k + (tree == 0), (tree + 1) * k) as i:
                    for u in range(U):
                        load_block(tree, i, u)

            def rows(ap, b):
                return ap[bass.ds(b * S, S), :].rearrange("(t p) d -> p t d", p=P)

            def load_final(i, u):
                b = i * U + u
                ge(sp, res_sb, T * (b - U + 1))
                for dst, src in ((qr, q_all), (kr, k_all)):
                    sp.dma_start(dst[u][:].rearrange("p t d -> p (t d)"),
                                 src[:, bass.ds(b, 1), :].rearrange("p o n -> p (o n)")).then_inc(qk_in[u], 16)
                sp.dma_start(x1r[u][:], rows(x1_dram, b)).then_inc(x1r_in[u], 16)

            def store_final(i, u):
                b = i * U + u
                sp.wait_ge(res_sb, T * (b + 1))
                sp.dma_start(rows(out, b), res[u][:]).then_inc(r_out[u], 16)

            sp.wait_ge(y_sb, TREES * BLOCKS)
            sp.wait_ge(q_in, 16 * NB * T)
            sp.wait_ge(k_in, 16 * NB * T)
            for u in range(U):
                load_final(0, u)
            with sp.Fori(1, NB // U) as i:
                for u in range(U):
                    store_final(i - 1, u)
                    load_final(i, u)
            for u in range(U):
                store_final(NB // U - 1, u)
            for u in range(U):
                sp.wait_ge(r_out[u], 16 * (NB // U))
            sp.wait_ge(zeroed, 16 * NB * TREES)

        @block.tensor
        def _(pe):
            mm = nc.tensor.matmul

            def tokens_T(b, u):
                ge(pe, xn_done, 2 * (b + 3))
                ge(pe, rk_sb, b - 1)
                ge(pe, count_up, b - 1)
                ge(pe, v_sb, b + 1)
                for t in range(T):
                    for c in range(C):
                        last = nc.tensor.transpose(G6[:, c * S + t * P:c * S + t * P + P],
                                                   xn[u][:, t, c * P:c * P + P], ident[:])
                last.then_inc(xnT_ps, 1)

            def project(ps, w, actT):
                for o in range(C):
                    for c in range(C):
                        last = mm(ps[:, o * S:o * S + S], w[:, c, o * P:o * P + P], actT(c),
                                  start=(c == 0), stop=(c == C - 1))
                return last

            def step(b, n, u):
                for j in range(PAIRS + LAG):
                    if j == 0 and has(b, 2):
                        tokens_T(b, u)
                    if j == 1 and has(b, 2):
                        pe.wait_ge(xnT_sb, b + 3)
                        ge(pe, ml_sb, b + 1)
                        ge(pe, kl_sb, b + 2)
                        project(G7, wq, lambda c: xnT[:, c * S:c * S + S]).then_inc(q_ps, 1)
                    if j == 2 and has(b, -1):
                        pe.wait_ge(aT_sb, b)
                        ge(pe, xnT_sb, b + 3 if has(b, 2) else NB)
                        ge(pe, rk_sb, b - 1)
                        ge(pe, count_up, b - 1)
                        for t in range(T):
                            for c in range(C):
                                last = mm(G6[:, t * D:t * D + D], aT[:, c * S + t * P:c * S + t * P + P],
                                          wo[:, c, :], start=(c == 0), stop=(c == C - 1))
                        last.then_inc(wo_ps, 1)
                    if j == 3 and has(b, 2):
                        pe.wait_ge(c_in[u], 16 * (n + 2))
                        pe.wait_ge(qh_sb, b + 3)
                        pe.wait_ge(ql_sb, b + 3)
                        project(G7, wk, lambda c: ct[u][:, c, :]).then_inc(k_ps, 1)
                    if j == 4 and has(b, 1):
                        pe.wait_ge(c_in[1 - u], 16 * (n + 1 + u))
                        ge(pe, x1_sb, b)
                        ge(pe, xnT_sb, b + 3 if has(b, 2) else NB)
                        for t in range(T):
                            for c in range(C):
                                last = mm(G6[:, t * D:t * D + D], ct[1 - u][:, c, t * P:t * P + P], wv[:, c, :],
                                          start=(c == 0), stop=(c == C - 1))
                        last.then_inc(v_ps, 1)
                    if j == 6 and has(b, -1):
                        pe.wait_ge(xn2_sb, 2 * b)
                        pe.wait_ge(kl_sb, b + 3 if has(b, 2) else NB)
                        for t in range(T):
                            for c in range(C):
                                last = nc.tensor.transpose(G7[:, c * S + t * P:c * S + t * P + P],
                                                           xn2s[1 - u][:, t, c * P:c * P + P], ident[:])
                        last.then_inc(xn2T_ps, 1)
                    if j == 8 and has(b, -1):
                        pe.wait_ge(xn2T_sb, b)
                        pe.wait_ge(v_sb, b + 2 if has(b, 1) else NB)
                        pe.wait_ge(x1_sb, b)
                        for t in range(T):
                            for c in range(C):
                                last = mm(G6[:, t * 64:t * 64 + TREES * NODES], xn2T[:, c * S + t * P:c * S + t * P + P],
                                          ndT[:, c, :], start=(c == 0), stop=(c == C - 1))
                        last.then_inc(node_ps, 1)
                    if j == 9 and has(b, 1):
                        pe.wait_ge(max_sb, PAIRS * (b + 2))
                        ge(pe, xn2T_sb, b)
                        ge(pe, kl_sb, b + 3 if has(b, 2) else NB)
                        for t in range(T):
                            last = nc.tensor.transpose(G7[0:NH, t * P:t * P + P], mneg[1 - u][:, t, :], ident[:])
                        last.then_inc(mT_ps, 1)
                    if j == 10 and has(b, -1):
                        pe.wait_ge(oh_sb, b)
                        o = oh[1 - u]
                        mm(G6[:, 128:128 + TL], trib[:], o[:, 0:TL], start=True, stop=True)
                        mm(G6[:, 192:192 + TL], trib[:], o[:, TL:2 * TL], start=True, stop=False)
                        mm(G6[:, 192:192 + TL], onesb[:], o[:, 0:TL], start=False, stop=True)
                        mm(G6[:, 256:256 + TL], onesb[:], o[:, 0:TL], start=True, stop=False)
                        mm(G6[:, 256:256 + TL], onesb[:], o[:, TL:2 * TL], start=False, stop=True
                           ).then_inc(rank_ps, 1)
                    if j < PAIRS and has(b, 1):
                        if j in (0, 4):
                            pe.wait_ge(stacked[j // 4][1 - u], 16 * STACKS * (n + 1 + u))
                        ge(pe, max_sb, PAIRS * (b + 1) + j)
                        for e in range(2):
                            h, ps, q, k = 2 * j + e, S_BANKS[:, e, :], q4[1 - u], k4[1 - u]
                            mm(ps[:, 0:S], q[0:KS, h, P:S], k[0:KS, h, :], start=True, stop=False)
                            mm(ps[:, P:S], identb[:], maskb[:], start=False, stop=True)
                            mm(ps[:, S:S + P], q[0:KS, h, 0:P], k[0:KS, h, 0:P], start=True, stop=False)
                            last = mm(ps[:, S:S + P], identb[:], maskb[:], start=False, stop=True)
                        last.then_inc(s_ps, 1)
                    p = j - LAG
                    if p >= 0 and has(b, 0):
                        if p == 0:
                            pe.wait_ge(m_row, 32 * (b + 1))
                        ge(pe, exp_sb, PAIRS * b + p)
                        for e in range(2):
                            h, ps, q, k = HORDER[2 * p + e], ST_BANKS[:, e, :], q4[u], k4[u]
                            mm(ps[:, 0:S], k[0:KM, h, 0:P], q[0:KM, h, :], start=True, stop=True)
                            last = mm(ps[:, S:S + P], k[0:KM, h, P:S], q[0:KM, h, P:S], start=True, stop=True)
                        last.then_inc(st_ps, 1)
                        if p % 2 and p > 1:
                            weigh(b, u, p // 2 - 1)
                if has(b, 0):
                    weigh(b, u, PAIRS // 2 - 1)

            def weigh(b, u, r):
                c, par = r // HQ, r % HQ
                pe.wait_ge(sel_sb, PAIRS * b + 2 * r + 2)
                if r == 0:
                    pe.wait_ge(v_sb, b + 1)
                    ge(pe, aT_sb, b)
                for ps, lhs in ((N_BANK, lambda kt, h: vp[u][:, kt, h, :]), (D_BANK, lambda kt, h: op[:, par, :])):
                    for kt in range(T):
                        for g in range(4):
                            t = 4 * r + g
                            last = mm(ps[32 * g:32 * g + 32, c * S + kt * P:c * S + S], lhs(kt, HORDER[t]),
                                      pt[:, t, 0:S] if kt == 0 else pt[:, t, S:S + P],
                                      start=(par == 0 and kt == 0), stop=(par == 1 and kt == 1))
                last.then_inc(pv_ps, 1)

            pe.wait_ge(consts, NCONST)
            pe.wait_ge(weights, 16 * 7)
            pipeline(step, pe)

            G = TREES * BLOCKS

            def block_T(i, u):
                g = i * U + u
                pe.wait_ge(xb_in[u], 16 * (i + 1))
                ge(pe, xbT_sb, g - 1)
                for c in range(C):
                    last = nc.tensor.transpose(banks[u % 2][:, c * P:c * P + P], xb[u][:, c * P:c * P + P], ident[:])
                last.then_inc(xbT_ps, 1)

            def block_h(i, u):
                g = i * U + u
                pe.wait_ge(xbT_sb, g + 1)
                pe.wait_ge(w_cp, g + 1)
                ge(pe, h_sb, g - 1)
                for c in range(C):
                    last = mm(banks[2 + u % 2][0:HID, 0:P], wb[u][:, c * HID:c * HID + HID],
                              xbT[u % 2][:, c * P:c * P + P], start=(c == 0), stop=(c == C - 1))
                last.then_inc(h_ps, 1)

            def block_out(i, u):
                g = i * U + u
                pe.wait_ge(h_sb, g + 1)
                ge(pe, y_sb, g - 1)
                mm(banks[4 + u % 2][:, 0:D], hT[u % 2][:], wb[u][0:HID + 1, C * HID:C * HID + D],
                   start=True, stop=True).then_inc(y_ps, 1)

            def blocks(i, more):
                for u in range(U):
                    if u + 2 < U or more:
                        block_T(i + (u + 2) // U, (u + 2) % U)
                    if u + 1 < U or more:
                        block_h(i + (u + 1) // U, (u + 1) % U)
                    block_out(i, u)

            pe.wait_ge(hT_one, 2)
            block_T(0, 0)
            block_T(0, 1)
            block_h(0, 0)
            blocks(0, True)
            with pe.Fori(1, G // U - 1) as i:
                blocks(i, True)
            blocks(G // U - 1, False)

            pe.wait_ge(y_sb, G)

            def transposes(i, u):
                b = i * U + u
                pe.wait_ge(qk_in[u], 32 * (i + 1))
                for ps, src, done, free in ((banks[0], qr[u], tq_ps, qT_sb), (banks[1], kr[u], tk_ps, kT_sb)):
                    ge(pe, free, b)
                    for t in range(T):
                        for c in range(C):
                            last = nc.tensor.transpose(ps[:, c * S + t * P:c * S + t * P + P],
                                                       src[:, t, c * P:c * P + P], ident[:])
                    last.then_inc(done, 1)

            def scores(i, u):
                b, w = i * U + u, u % 2
                pe.wait_ge(qT_sb, b + 1)
                pe.wait_ge(kT_sb, b + 1)
                ge(pe, e2_sb, T * (b - 1))
                for t in range(T):
                    for c in range(C):
                        last = mm(banks[2 + w][:, t * S:t * S + S], qT[w][:, c * S + t * P:c * S + t * P + P],
                                  kT[w][:, c * S:c * S + S], start=(c == 0), stop=(c == C - 1))
                last.then_inc(s2_ps, 1)

            def probs_T(i, u):
                b, w = i * U + u, u % 2
                pe.wait_ge(e2_sb, T * (b + 1))
                ge(pe, pT_sb, b - 1)
                for qt in range(T):
                    for kt in range(T):
                        last = nc.tensor.transpose(banks[4 + w][:, kt * S + qt * P:kt * S + qt * P + P],
                                                   pr[w][:, qt, kt * P:kt * P + P], ident[:])
                last.then_inc(pT_ps, 1)

            def values(i, u):
                b, w = i * U + u, u % 2
                pe.wait_ge(pT_sb, b + 1)
                pe.wait_ge(v_in[u], 32 * (i + 1))
                ge(pe, res_sb, T * (b - 1))
                for t in range(T):
                    for kt in range(T):
                        last = mm(banks[6 + w][:, t * D:t * D + D], prT[w][:, kt, t * P:t * P + P], vr[u][:, kt, :],
                                  start=(kt == 0), stop=(kt == T - 1))
                last.then_inc(o_ps, 1)

            def finals(i, more):
                for u in range(U):
                    if u + 2 < U or more:
                        transposes(i + (u + 2) // U, (u + 2) % U)
                    probs_T(i, u)
                    if u + 1 < U or more:
                        scores(i + (u + 1) // U, (u + 1) % U)
                    values(i, u)

            transposes(0, 0)
            scores(0, 0)
            transposes(0, 1)
            finals(0, True)
            with pe.Fori(1, NB // U - 1) as i:
                finals(i, True)
            finals(NB // U - 1, False)

        @block.scalar
        def _(act):
            def step(b, n, u):
                for j in range(PAIRS + LAG):
                    p = j
                    if p == 0 and has(b, 2):
                        act.wait_ge(xnT_ps, b + 3)
                        ge(act, q_ps, b + 2)
                        nc.scalar.copy(xnT[:], G6[:]).then_inc(xnT_sb, 1)
                    if p == 1 and has(b, 2):
                        act.wait_ge(q_ps, b + 3)
                        ge(act, unloaded[u], 64 * (n + 1))
                        nc.scalar.copy(q_hi[u][:].rearrange("p c k -> p (c k)"), G7[:]).then_inc(qh_sb, 1)
                    if p == 3 and has(b, 2):
                        act.wait_ge(k_ps, b + 3)
                        nc.scalar.copy(k_hi[u][:].rearrange("p c k -> p (c k)"), G7[:]).then_inc(kh_sb, 1)
                    if p == 4 and has(b, 1):
                        act.wait_ge(v_ps, b + 2)
                        ge(act, pv_ps, 4 * b)
                        for par in range(HQ):
                            o = vp[1 - u][:].rearrange("p t (j e) c -> p (t j) e c", e=HQ)[:, :, par, DK * par:DK * par + DK]
                            i = G6[:].rearrange("p (j e c) -> p j e c", e=HQ, c=DK)[:, :, par, :]
                            last = nc.scalar.copy(o, i)
                        last.then_inc(v_sb, 1)
                    if p == 7 and has(b, -1):
                        act.wait_ge(xn2T_ps, b)
                        ge(act, node_ps, b - 1)
                        nc.scalar.copy(xn2T[:], G7[:]).then_inc(xn2T_sb, 1)
                    p = j - LAG
                    if p >= 0 and has(b, 0):
                        act.wait_ge(st_ps, PAIRS * b + p + 1)
                        if p % 2 == 0:
                            ge(act, pv_ps, 4 * (b - 1) + p // 2 + 1)
                        nc.scalar.activation(pt[:, 2 * p:2 * p + 2, :], ST_BANKS[:, :, 0:S + P], ACT.Exp,
                                             scale=SC).then_inc(exp_sb, 1)

            pipeline(step, act)

            act.wait_ge(hT_one, 2)

            def copy_xT(i, u):
                g = i * U + u
                act.wait_ge(xbT_ps, g + 1)
                ge(act, h_ps, g - 1)
                nc.scalar.copy(xbT[u % 2][:], banks[u % 2][:, 0:D]).then_inc(xbT_sb, 1)

            def relu(i, u):
                g = i * U + u
                act.wait_ge(h_ps, g + 1)
                ge(act, y_ps, g - 1)
                nc.scalar.activation(hT[u % 2][0:HID, :], banks[2 + u % 2][0:HID, 0:P], ACT.Relu,
                                     bias=wb[u][0:HID, WC - 1:WC]).then_inc(h_sb, 1)

            def store(tree, i, u):
                g = i * U + u
                act.wait_ge(y_sb, g + 1)
                act.dma_start(ys_dram[tree][bass.ds((g - tree * BLOCKS) * RUN, RUN), :], yb[u][:]).then_inc(y_out[u], 16)

            def blocks(tree, i, first=False, after=True):
                for u in range(U):
                    if u + 2 < U or after:
                        copy_xT(i + (u + 2) // U, (u + 2) % U)
                    if u + 1 < U or after:
                        relu(i + (u + 1) // U, (u + 1) % U)
                    if u > 0:
                        store(tree, i, u - 1)
                    elif not first or tree > 0:
                        store(tree - first, i - 1, U - 1)

            copy_xT(0, 0)
            copy_xT(0, 1)
            relu(0, 0)
            for tree in range(TREES):
                k0, k1 = tree * BLOCKS // U, (tree + 1) * BLOCKS // U
                end = k1 - (tree == TREES - 1)
                blocks(tree, k0, first=True)
                with act.Fori(k0 + 1, end) as i:
                    blocks(tree, i)
            blocks(TREES - 1, k1 - 1, after=False)
            store(TREES - 1, k1 - 1, U - 1)

            def copy_qT(i, u):
                b = i * U + u
                act.wait_ge(tq_ps, b + 1)
                ge(act, s2_ps, b - 1)
                nc.scalar.copy(qT[u % 2][:], banks[0][:]).then_inc(qT_sb, 1)

            def exps(i, u):
                b, w = i * U + u, u % 2
                act.wait_ge(mb2_sb, b + 1)
                ge(act, pT_ps, b - 1)
                ge(act, rs2_sb, b - 1)
                for t in range(T):
                    nc.scalar.activation(pr[w][:, t, :], banks[2 + w][:, t * S:t * S + S], ACT.Exp, scale=SC2,
                                         bias=mb2[w][:, t:t + 1], accum_out=sum2[w][:, t:t + 1]).then_inc(e2_sb, 1)

            def finals(i, more):
                for u in range(U):
                    if u + 2 < U or more:
                        copy_qT(i + (u + 2) // U, (u + 2) % U)
                    if u + 1 < U or more:
                        exps(i + (u + 1) // U, (u + 1) % U)

            copy_qT(0, 0)
            exps(0, 0)
            copy_qT(0, 1)
            finals(0, True)
            with act.Fori(1, NB // U - 1) as i:
                finals(i, True)
            finals(NB // U - 1, False)

        @block.vector
        def _(v):
            def norm_in(b, n, s):
                v.wait_ge(x_in[s], 16 * (n + 1))
                for t in range(T):
                    nc.vector.bn_stats(st1[:, t, :], xt[s][:, t, :]).then_inc(stats1, 1)
                v.wait_ge(stats1, T * (b + 1))
                ge(v, rstd1, b)
                apart(v)
                for t in range(T):
                    nc.vector.bn_aggr(mv1[:, t, :], st1[:, t, :]).then_inc(aggr1, 1)

            def norm_out(b, n, s):
                v.wait_ge(rstd1, b + 1)
                ge(v, xnT_ps, b - 1)
                for t in range(T):
                    nc.vector.tensor_scalar(xn[s][:, t, :], xt[s][:, t, :], mv1[:, t, 0:1], rs1[:, t:t + 1],
                                            ALU.subtract, ALU.mult).then_inc(xn_done, 1)

            def step(b, n, u):
                for j in range(PAIRS + LAG):
                    p = j
                    if p == 0 and has(b, -1):
                        v.wait_ge(pv_ps, 4 * b)
                        nc.vector.reciprocal(rden[:], D_BANK[:]).then_inc(rden_sb, 1)
                        v.wait_ge(rden_sb, b)
                        ge(v, wo_ps, b - 1)
                        nc.vector.tensor_tensor(aT[:], N_BANK[:], rden[:], ALU.mult).then_inc(aT_sb, 1)
                    if p == 2 and has(b, 2):
                        v.wait_ge(qh_sb, b + 3)
                        nc.vector.tensor_tensor(q_lo[u][:].rearrange("p c k -> p (c k)"), G7[:],
                                                q_hi[u][:].bitcast(FP).rearrange("p c k -> p (c k)"),
                                                ALU.subtract).then_inc(ql_sb, 1)
                    if p == 3 and has(b, -1):
                        v.wait_ge(wo_ps, b)
                        v.wait_ge(xr_in[1 - u], 16 * (n + u))
                        ge(v, x1_out[1 - u], 16 * (n - 1 + u))
                        ge(v, xn2_sb, T * (b - 1))
                        nc.vector.tensor_tensor(x1[1 - u][:].rearrange("p t d -> p (t d)"), G6[:],
                                                xr[1 - u][:].rearrange("p t d -> p (t d)"), ALU.add).then_inc(x1_sb, 1)
                        v.wait_ge(x1_sb, b)
                        for t in range(T):
                            nc.vector.bn_stats(st2[:, t, :], x1[1 - u][:, t, :]).then_inc(stats2, 1)
                        v.wait_ge(stats2, T * b)
                        ge(v, rstd2, b - 1)
                        apart(v)
                        for t in range(T):
                            nc.vector.bn_aggr(mv2[:, t, :], st2[:, t, :]).then_inc(aggr2, 1)
                    if p == 4 and has(b, 2):
                        v.wait_ge(kh_sb, b + 3)
                        nc.vector.tensor_tensor(k_lo[u][:].rearrange("p c k -> p (c k)"), G7[:],
                                                k_hi[u][:].bitcast(FP).rearrange("p c k -> p (c k)"),
                                                ALU.subtract).then_inc(kl_sb, 1)
                    if p == 5 and has(b, -1):
                        v.wait_ge(rstd2, b)
                        ge(v, xn2T_ps, b - 2)
                        ge(v, xn2_kept, b - 2)
                        for t in range(T):
                            nc.vector.tensor_scalar(xn2s[1 - u][:, t, :], x1[1 - u][:, t, :], mv2[:, t, 0:1],
                                                    rs2[:, t:t + 1], ALU.subtract, ALU.mult).then_inc(xn2_sb, 1)
                    if p == 6 and has(b, 3):
                        norm_in(b + 3, *norm_slot(b, n, u))
                    if p == 8 and has(b, 3):
                        norm_out(b + 3, *norm_slot(b, n, u))
                    if p == 8 and has(b, -1):
                        tree(b, n, u)
                    if p == 9 and has(b, 1):
                        v.wait_ge(mT_ps, b + 2)
                        ge(v, m_row, 32 * (b + 1))
                        nc.vector.tensor_copy(m_hi[:], G7[0:NH, 0:S]).then_inc(mh_sb, 1)
                        v.wait_ge(mh_sb, b + 2)
                        nc.vector.tensor_tensor(m_lo[:], G7[0:NH, 0:S], m_hi[:].bitcast(FP), ALU.subtract).then_inc(ml_sb, 1)
                    if p == 10 and has(b, -1):
                        ranks(b, n, u)
                    if p < PAIRS and has(b, 1):
                        v.wait_ge(s_ps, PAIRS * (b + 1) + p + 1)
                        if p == 0:
                            ge(v, mT_ps, b)
                        for t, cols in ((1, slice(0, S)), (0, slice(S, S + P))):
                            last = nc.vector.tensor_reduce(mneg[1 - u][:, t, 2 * p:2 * p + 2], S_BANKS[:, :, cols],
                                                           axis=AX.X, op=ALU.max, negate=True)
                        last.then_inc(max_sb, 1)

            def norm_slot(b, n, u):
                return n + 1 + u, 1 - u

            def tree(b, n, u):
                v.wait_ge(node_ps, b)
                nc.vector.tensor_tensor(sc[:], G6[:, 0:128].rearrange("p (t m) -> p t m", t=T)[:, :, 0:TREES * NODES],
                                        ndb[:], ALU.add).then_inc(sc_sb, 1)
                v.wait_ge(sc_sb, b)
                scr = sc[:].rearrange("p t (r m) -> p (t r) m", m=NODES)
                nc.vector.tensor_scalar(g2[:, :, :, 1], scr, 0.0, None, ALU.is_ge).then_inc(g_step, 1)
                nc.vector.tensor_scalar(g2[:, :, :, 0], scr, 0.0, None, ALU.is_lt).then_inc(g_step, 1)
                v.wait_ge(g_step, 2 * b)
                R = T * TREES
                src = g2[:, :, 0, :]
                for lvl, (dst, done) in enumerate(((l2[:], lvl2), (l3[:], lvl3),
                                                   (oh[1 - u][:].rearrange("p (r l) -> p r l", l=LEAVES), oh_sb))):
                    m = 2 << lvl
                    if done is oh_sb:
                        ge(v, oh_kept, b - 2)
                        ge(v, rank_ps, b - 2)
                        ge(v, rp_sb, b - 2)
                    nc.vector.tensor_tensor(dst.rearrange("p r (m e) -> p r m e", e=2),
                                            src.unsqueeze(3).to_broadcast([P, R, m, 2]),
                                            g2[:, :, m - 1:2 * m - 1, :], ALU.mult).then_inc(done, 1)
                    v.wait_ge(done, b)
                    src = dst

            def ranks(b, n, u):
                v.wait_ge(rank_ps, b)
                ge(v, count_up, b - 1)
                nc.vector.tensor_tensor(rk[:], G6[:, 128:256].rearrange("p (t m) -> p t m", t=T)[:, :, 0:TL],
                                        count[:].unsqueeze(1).to_broadcast([P, T, TL]), ALU.add).then_inc(rk_sb, 1)
                v.wait_ge(rk_sb, b)
                nc.vector.tensor_tensor(rp[:].rearrange("p t m -> p (t m)"), rk[:].rearrange("p t m -> p (t m)"),
                                        oh[1 - u][:], ALU.mult).then_inc(rp_sb, 1)
                nc.vector.tensor_tensor(count[:], count[:], G6[:, 256:256 + TL], ALU.add).then_inc(count_up, 1)
                v.wait_ge(rp_sb, b)
                nc.vector.tensor_reduce(rank[:, bass.ds(b - 1, 1), :], rp[:].rearrange("p t (r l) -> p (t r) l", l=LEAVES),
                                        axis=AX.X, op=ALU.add).then_inc(rank_kept, 1)
                nc.vector.tensor_copy(onehot[:, bass.ds(b - 1, 1), :], oh[1 - u][:]).then_inc(oh_kept, 1)

            for s in range(2):
                nc.vector.memset(k4[s][KS:KM, :, :].bitcast(FP), 1.0).then_inc(consts, 1)
            v.wait_ge(consts, NCONST)
            v.wait_ge(weights, 16 * 7)
            for b0 in range(1):
                norm_in(b0, 0, b0)
                norm_out(b0, 0, b0)
            pipeline(step, v)

            steps = [0]

            def done(ins):
                steps[0] += 1
                ins.then_inc(route, 1)
                v.wait_ge(route, steps[0])

            v.wait_ge(count_up, NB)
            v.wait_ge(rank_kept, NB)
            v.wait_ge(oh_kept, NB)
            v.wait_ge(iotas, 2)
            done(nc.vector.tensor_copy(iota_t[:], iota_i[:, 0:NB * T]))
            done(nc.vector.tensor_copy(iota_b[:], iota_i[:, NB * T:]))
            done(nc.vector.tensor_tensor(cmp_t[:], count[:].unsqueeze(2).to_broadcast([P, TL, NB * T]),
                                         iota_t[:].unsqueeze(1).to_broadcast([P, TL, NB * T]), ALU.is_gt))
            done(nc.vector.tensor_reduce(nblk[0][:].rearrange("p r l -> p (r l)"), cmp_t[:], axis=AX.X, op=ALU.add))
            for k in range(4):
                w, a, o = 1 << k, nblk[k], nblk[k + 1]
                done(nc.vector.tensor_tensor(o[:, :, w:], a[:, :, w:], a[:, :, 0:LEAVES - w], ALU.add))
                done(nc.vector.tensor_copy(o[:, :, 0:w], a[:, :, 0:w]))
            done(nc.vector.tensor_tensor(offs[:], nblk[4][:], nblk[0][:], ALU.subtract))
            for r in range(TREES):
                done(nc.vector.tensor_scalar(nblk[1][:, r, :], offs[:, r, :], float(RUN), None, ALU.mult))
            done(nc.vector.tensor_tensor(tmp_p[:], onehot[:].rearrange("p b (t m) -> p (b t) m", t=T),
                                         nblk[1][:].rearrange("p r l -> p (r l)").unsqueeze(1).to_broadcast([P, NB * T, TL]),
                                         ALU.mult))
            done(nc.vector.tensor_reduce(placef[:].rearrange("p t r -> p (t r)"),
                                         tmp_p[:].rearrange("p t (r l) -> p (t r) l", l=LEAVES), axis=AX.X, op=ALU.add))
            nc.vector.tensor_tensor(place[:], placef[:].rearrange("p t r -> p (t r)"),
                                    rank[:].rearrange("p b m -> p (b m)"), ALU.add).then_inc(placed, 1)
            for r in range(TREES):
                last = nc.vector.tensor_tensor(cmp_b[:, r], iota_b[:].unsqueeze(2).to_broadcast([P, BLOCKS, LEAVES]),
                                               nblk[4][:, r, :].unsqueeze(1).to_broadcast([P, BLOCKS, LEAVES]), ALU.is_ge)
                done(last)
            done(nc.vector.tensor_reduce(leaff[:], cmp_b[:].rearrange("p r b l -> p (r b) l"), axis=AX.X, op=ALU.add))
            for r in range(TREES):
                bs = slice(r * BLOCKS, (r + 1) * BLOCKS)
                last = nc.vector.tensor_scalar(blockleaf[:, bs], leaff[:, bs], float(LEAVES - 1), float(r * LEAVES),
                                               ALU.min, ALU.add)
            last.then_inc(leaves, 1)

            for u in range(2):
                nc.vector.memset(hT[u][HID:HID + 1, :], 1.0).then_inc(hT_one, 1)
            v.wait_ge(wt_late, 16 * TREES)
            v.wait_ge(leaves, 1)

            def take_weights(i, u):
                g = i * U + u
                leaf = v.value_load(blockleaf[0:1, bass.ds(g, 1)], min_val=0, max_val=TL - 1)
                ge(v, y_ps, g - U + 1)
                nc.vector.tensor_copy(wb[u][:], wl[:, bass.ds(leaf, 1), :].rearrange("p o n -> p (o n)")).then_inc(w_cp, 1)

            def copy_y(i, u):
                v.wait_ge(y_ps, i * U + u + 1)
                ge(v, y_out[u], 16 * i)
                nc.vector.tensor_copy(yb[u][:], banks[4 + u % 2][:, 0:D]).then_inc(y_sb, 1)

            for u in range(U):
                take_weights(0, u)
            k = TREES * BLOCKS // U
            for u in range(U):
                copy_y(0, u)
                take_weights(1, u)
            with v.Fori(1, k - 1) as i:
                for u in range(U):
                    copy_y(i, u)
                    take_weights(i + 1, u)
            for u in range(U):
                copy_y(k - 1, u)

            def copy_kT(i, u):
                b = i * U + u
                v.wait_ge(tk_ps, b + 1)
                ge(v, s2_ps, b - 1)
                nc.vector.tensor_copy(kT[u % 2][:], banks[1][:]).then_inc(kT_sb, 1)

            def maxima(i, u):
                b, w = i * U + u, u % 2
                v.wait_ge(s2_ps, b + 1)
                nc.vector.tensor_reduce(m2[w][:], banks[2 + w][:].rearrange("p (t k) -> p t k", t=T), axis=AX.X,
                                        op=ALU.max, negate=True).then_inc(m2_sb, 1)
                v.wait_ge(m2_sb, b + 1)
                ge(v, e2_sb, T * (b - 1))
                nc.vector.tensor_scalar(mb2[w][:], m2[w][:], SC2, None, ALU.mult).then_inc(mb2_sb, 1)

            def copy_pT(i, u):
                b, w = i * U + u, u % 2
                v.wait_ge(pT_ps, b + 1)
                ge(v, o_ps, b - 1)
                nc.vector.tensor_copy(prT[w][:].rearrange("p t k -> p (t k)"), banks[4 + w][:]).then_inc(pT_sb, 1)
                nc.vector.reciprocal(rsum2[w][:], sum2[w][:]).then_inc(rs2_sb, 1)

            def finish(i, u):
                b, w = i * U + u, u % 2
                v.wait_ge(rs2_sb, b + 1)
                v.wait_ge(o_ps, b + 1)
                v.wait_ge(x1r_in[u], 16 * (i + 1))
                ge(v, r_out[u], 16 * i)
                for t in range(T):
                    nc.vector.scalar_tensor_tensor(res[u][:, t, :], banks[6 + w][:, t * D:t * D + D],
                                                   rsum2[w][:, t:t + 1], x1r[u][:, t, :],
                                                   ALU.mult, ALU.add).then_inc(res_sb, 1)

            def finals(i, more):
                for u in range(U):
                    if u + 2 < U or more:
                        copy_kT(i + (u + 2) // U, (u + 2) % U)
                    copy_pT(i, u)
                    if u + 1 < U or more:
                        maxima(i + (u + 1) // U, (u + 1) % U)
                    finish(i, u)

            copy_kT(0, 0)
            maxima(0, 0)
            copy_kT(0, 1)
            finals(0, True)
            with v.Fori(1, NB // U - 1) as i:
                finals(i, True)
            finals(NB // U - 1, False)

        @block.gpsimd
        def _(gp):
            pool = nc.gpsimd
            for tile, value in ((ident, 0.0), (maskb, 0.0), (trib, 1.0), (onesb, 1.0), (mhalf, -0.5), (zero, 0.0),
                                (count, 0.0), (op, 0.0), (vp[0], 0.0), (vp[1], 0.0)):
                pool.memset(tile[:], value).then_inc(consts, 1)
            gp.wait_ge(consts, 12)
            pool.affine_select(out=ident[:], in_=ident[:], compare_op=ALU.not_equal, fill=1.0, base=0,
                               pattern=[[-1, P]], channel_multiplier=1).then_inc(consts, 1)
            pool.affine_select(out=maskb[:], in_=maskb[:], compare_op=ALU.is_ge, fill=NEG, base=0,
                               pattern=[[-1, P]], channel_multiplier=1).then_inc(consts, 1)
            pool.affine_select(out=trib[:], in_=trib[:], compare_op=ALU.is_gt, fill=0.0, base=0,
                               pattern=[[1, P]], channel_multiplier=-1).then_inc(consts, 1)
            for par in range(HQ):
                pool.memset(op[:, par, DK * par:DK * par + DK], 1.0).then_inc(consts, 1)
            gp.wait_ge(consts, 17)
            pool.tensor_copy(identb[:], ident[:]).then_inc(consts, 1)
            gp.wait_ge(consts, NCONST)

            def rsqrt(b, aggr, mv, ve, var_sem, rs, rstd_sem, prev_read):
                gp.wait_ge(aggr, T * (b + 1))
                ge(gp, *prev_read)
                apart(gp)
                pool.tensor_scalar(ve[:], mv[:, :, 1], EPS, None, ALU.add).then_inc(var_sem, 1)
                gp.wait_ge(var_sem, b + 1)
                pool.tensor_tensor(rs[:], ve[:], mhalf[:], ALU.pow).then_inc(rstd_sem, 1)

            def step(b, n, u):
                for j in range(PAIRS + LAG):
                    p = j
                    if p == 4 and has(b, -1):
                        rsqrt(b - 1, aggr2, mv2, ve2, var2, rs2, rstd2, (xn2_sb, T * (b - 1)))
                    if p == 7 and has(b, 3):
                        rsqrt(b + 3, aggr1, mv1, ve1, var1, rs1, rstd1, (xn_done, T * (b + 3)))
                    if p == 9 and has(b, -1):
                        gp.wait_ge(xn2_sb, T * b)
                        pool.tensor_copy(xn2[:, bass.ds(b - 1, 1), :],
                                         xn2s[1 - u][:].rearrange("p t d -> p (t d)")).then_inc(xn2_kept, 1)
                    p = j - LAG
                    if p >= 0 and has(b, 0):
                        gp.wait_ge(exp_sb, PAIRS * b + p + 1)
                        apart(gp)
                        for cols in (slice(0, P), slice(S, S + P)):
                            dg = pt[:, 2 * p:2 * p + 2, cols]
                            last = pool.affine_select(out=dg, in_=dg, compare_op=ALU.is_ge, fill=0.0, base=0,
                                                      pattern=[[0, 2], [1, P]], channel_multiplier=-1)
                        last.then_inc(sel_sb, 1)

            rsqrt(0, aggr1, mv1, ve1, var1, rs1, rstd1, (xn_done, 0))
            pipeline(step, gp)

            gp.wait_ge(count_up, NB)
            for s in range(2):
                gp.wait_ge(x1_out[s], 16 * (NB // 2))
            pool.iota(iota_i[:, 0:NB * T], pattern=[[P, NB * T]], base=0, channel_multiplier=0).then_inc(iotas, 1)
            pool.iota(iota_i[:, NB * T:], pattern=[[1, BLOCKS]], base=0, channel_multiplier=0).then_inc(iotas, 1)
            gp.wait_ge(placed, 1)
            gp.wait_ge(zeroed, 16 * NB * TREES)
            gp.wait_ge(xn2_kept, NB)

            def scatter(tree):
                for t in range(NB * T):
                    k = t * TREES + tree
                    gp.indirect_dma_start(xs_dram[tree], bass.IndirectOffsetOnAxis(ap=place[:, k:k + 1], axis=0),
                                          xn2[:, t // T, (t % T) * D:(t % T) * D + D], None).then_inc(scat[tree], 16)

            for tree in range(TREES):
                scatter(tree)

            for tree, (rows_all, done) in enumerate(((q_all, q_in), (k_all, k_in))):
                for s in range(U):
                    gp.wait_ge(y_out[s], 16 * (tree + 1) * BLOCKS // U)
                if rows_all is xn2:
                    for s in range(TREES):
                        gp.wait_ge(scat[s], 16 * NB * T)
                for t in range(NB * T):
                    m = t * TREES + tree
                    gp.indirect_dma_start(rows_all[:, t // T, (t % T) * D:(t % T) * D + D], None, ys_dram[tree],
                                          bass.IndirectOffsetOnAxis(ap=place[:, m:m + 1], axis=0)).then_inc(done, 16)
            for s in range(U):
                gp.wait_ge(y_out[s], 16 * TREES * BLOCKS // U)

            def gather(i, u):
                b = i * U + u
                ge(gp, o_ps, b - U + 1)
                ge(gp, v_in[u], 32 * i)
                pool.tensor_copy(pidx[u][:], place[:, bass.ds(b * T * TREES, T * TREES)]).then_inc(idx_cp, 1)
                gp.wait_ge(idx_cp, b + 1)
                apart(gp)
                for t in range(T):
                    m = t * TREES + TREES - 1
                    gp.indirect_dma_start(vr[u][:, t, :], None, ys_dram[TREES - 1],
                                          bass.IndirectOffsetOnAxis(ap=pidx[u][:, m:m + 1], axis=0)
                                          ).then_inc(v_in[u], 16)

            for u in range(U):
                gather(0, u)
            with gp.Fori(1, NB // U) as i:
                for u in range(U):
                    gather(i, u)


def kernel(**a):
    import concourse.bacc as bacc
    from concourse.bass_utils import run_bass_kernel_spmd as run

    a = {k: np.asarray(v) for k, v in a.items()}
    n = {k: a[f"L0_xattn_{k}"] for k in ("w_q", "w_k", "w_v", "w_o")}
    f = {k: np.stack([a[f"L0_ffn_{t}_{k}"] for t in "qkv"]) for k in ("node_w", "node_b", "w1", "b1", "w2", "b2")}
    leafw = np.zeros((TREES, P, LEAVES, WC), np.float32)
    for c in range(C):
        leafw[:, :, :, c * HID:(c + 1) * HID] = f["w1"][:, :, c * P:(c + 1) * P, :].transpose(0, 2, 1, 3)
    leafw[:, 0:HID, :, C * HID:C * HID + D] = f["w2"].transpose(0, 2, 1, 3)
    leafw[:, HID, :, C * HID:C * HID + D] = f["b2"]
    leafw[:, 0:HID, :, WC - 1] = f["b1"].transpose(0, 2, 1)

    def by_dim(w):
        return w.reshape(D, C, NH // C, DK).transpose(0, 1, 3, 2).reshape(D, D)

    arrays = {
        "x": a["x"].reshape(NTOK, D),
        "ctxT": a["ctx_1024"].transpose(0, 2, 1).reshape(NB * D, S),
        "wqT": by_dim(n["w_q"].T), "wkT": by_dim(n["w_k"].T), "wvT": n["w_v"].T, "woT": n["w_o"].T,
        "nodeT": f["node_w"].reshape(TREES * NODES, D).T,
        "nodeb": f["node_b"].reshape(1, TREES * NODES),
        "leafw": leafw,
    }
    arrays = {k: np.ascontiguousarray(v) for k, v in arrays.items()}
    nc = bacc.Bacc("TRN2", target_bir_lowering=False, num_devices=1)
    args = {k: nc.dram_tensor(k, v.shape, mybir.dt.from_np(v.dtype), kind="ExternalInput").ap()
            for k, v in arrays.items()}
    out = nc.dram_tensor("out", (NTOK, D), FP, kind="ExternalOutput").ap()
    build(nc, **args, out=out)
    r = run(nc, [arrays], core_ids=[0])
    return r.results[0]["out"].reshape(NB, S, D)
```

```python
from contextlib import ExitStack

import concourse.bass as bass
import numpy as np
from concourse import mybir

FP, BF, FR, I32 = mybir.dt.float32, mybir.dt.bfloat16, mybir.dt.float32r, mybir.dt.int32
ALU, ACT, AX = mybir.AluOpType, mybir.ActivationFunctionType, mybir.AxisListType

P = 128
NB, S, D = 16, 256, 256
T = S // P
C = D // P
NH = 16
DK = D // NH
HQ = 32 // DK
PARTS = 4
KS = PARTS * DK
KM = KS + 2
TREES, LEAVES, NODES, HID = 3, 16, 15, 64
TL = TREES * LEAVES
RUN = P
NTOK = NB * S
BLOCKS = (NTOK - LEAVES) // RUN + LEAVES
BLOCKS += -BLOCKS % 8
ROWS = BLOCKS * RUN
EPS = 1e-5
NEG = -3.0e38
SC = DK ** -0.5
SC2 = D ** -0.5
PAIRS = NH // 2
STACKS = 5
LAG = 3
U = 4
UB = 8
UP = UB // 2
HORDER = [8 * c + 2 * g + par for c in range(C) for par in range(HQ) for g in range(4)]


def build(nc, x, ctxT, wqT, wkT, wvT, woT, nodeT, nodeb, leafw1, leafw2, out):
    ctx = ExitStack()
    scope = ExitStack()
    with ctx:
        def sb(name, shape, dt=FP, at=ctx):
            return at.enter_context(nc.sbuf_tensor(name, shape, dt))

        def sem(name):
            return ctx.enter_context(nc.semaphore(name))

        def sems(name, n=2):
            return [sem(f"{name}{i}") for i in range(n)]

        xs_dram = [nc.dram_tensor(f"xs_dram{t}", [ROWS, D], FP, kind="Internal").ap() for t in range(TREES)]
        parts_dram = [nc.dram_tensor(f"parts_dram{i}", [2, C, 2, P, S], FP, kind="Internal").ap() for i in range(2)]
        ys_dram = [nc.dram_tensor(f"ys_dram{t}", [ROWS, D], FP, kind="Internal").ap() for t in range(TREES)]
        x1_dram = nc.dram_tensor("x1_dram", [NTOK, D], FP, kind="Internal").ap()

        ident = sb("ident", [P, P])
        identb = sb("identb", [P, P], BF)
        mask2 = sb("mask2", [P, 2 * P], BF)
        trib = sb("trib", [P, P], BF)
        onesb = sb("onesb", [P, P], BF)
        xn2 = sb("xn2", [P, NB, T * D])
        onehot = sb("onehot", [P, NB, T * TL], BF)
        rank = sb("rank", [P, NB, T * TREES])
        count = sb("count", [P, TL])
        PAD = LEAVES // 2
        run = [sb(f"run{i}", [P, TREES, PAD + LEAVES]) for i in range(5)]
        count_i = [sb(f"count_i{i}", [P, TREES, LEAVES], I32) for i in range(3)]
        place = sb("place", [P, NB * T * TREES], I32)
        blockleaf = sb("blockleaf", [P, TREES * BLOCKS], I32)
        pairs = [ctx.enter_context(nc.psum_tensor(f"banks{i}", [P, 2, 512], FP)) for i in range(4)]
        banks = [pairs[i // 2][:, i % 2, :] for i in range(8)]

        def at(name, shape, dt=FP):
            return sb(name, shape, dt, scope)

        wq, wk, wv, wo = (at(n, [P, C, D]) for n in ("wq", "wk", "wv", "wo"))
        ndT = at("ndT", [P, C, TREES * NODES])
        ndb = at("ndb", [P, T, TREES * NODES])
        zero = at("zero", [P, D])
        xt = [at(f"xt{i}", [P, T, D]) for i in range(2)]
        ct = [at(f"ct{i}", [P, C, S]) for i in range(2)]
        xr = [at(f"xr{i}", [P, T, D]) for i in range(2)]
        xn = [at(f"xn{i}", [P, T, D]) for i in range(2)]
        xnT = at("xnT", [P, C * S])
        q_hi, q_lo, k_hi, k_lo = ([at(f"{n}{i}", [P, C, S], FR) for i in range(2)]
                                  for n in ("q_hi", "q_lo", "k_hi", "k_lo"))
        q4 = [at(f"q4{i}", [KM, NH, S], FR) for i in range(2)]
        k4 = [at(f"k4{i}", [KM, NH, S], FR) for i in range(2)]
        vp = [at(f"vp{i}", [P, T, NH, 32]) for i in range(2)]
        pt = at("pt", [P, NH, 384])
        mneg = [at(f"mneg{i}", [P, T, NH]) for i in range(2)]
        m_hi, m_lo = at("m_hi", [NH, S], FR), at("m_lo", [NH, S], FR)
        nd = [at(f"nd{i}", [P, C * S]) for i in range(HQ)]
        rden = [at(f"rden{i}", [P, T * C * 4]) for i in range(HQ)]
        arow = at("arow", [P, T, D])
        aT = at("aT", [P, C * S])
        x1 = [at(f"x1{i}", [P, T, D]) for i in range(2)]
        xn2s = [at(f"xn2s{i}", [P, T, D]) for i in range(2)]
        xn2T = at("xn2T", [P, C * S])
        st1, st2 = at("st1", [P, T, 6]), at("st2", [P, T, 6])
        mv1, mv2 = at("mv1", [P, T, 2]), at("mv2", [P, T, 2])
        ve1, ve2, rs1, rs2 = (at(n, [P, T]) for n in ("ve1", "ve2", "rs1", "rs2"))
        mhalf = at("mhalf", [P, T])
        sc = at("sc", [P, T, TREES * NODES])
        g2 = at("g2", [P, T * TREES, NODES, 2])
        l2, l3 = at("l2", [P, T * TREES, 4]), at("l3", [P, T * TREES, 8])
        oh = [at(f"oh{i}", [P, T * TREES * LEAVES], BF) for i in range(2)]
        rk = at("rk", [P, T, TL])
        rp = at("rp", [P, T, TL])

        scope.close()
        wb1 = [sb(f"wb1_{i}", [P, C * HID]) for i in range(UB)]
        wb2 = [sb(f"wb2_{i}", [HID + 1, D + 1]) for i in range(UB)]
        xb = [sb(f"xb{i}", [P, 2, D]) for i in range(UP)]
        xbT = [sb(f"xbT{i}", [P, D]) for i in range(2)]
        hT = [sb(f"hT{i}", [HID + 1, P]) for i in range(2)]
        yb = [sb(f"yb{i}", [P, 2, D]) for i in range(UP)]
        iota_i = sb("iota_i", [P, BLOCKS], I32)
        q_all = sb("q_all", [P, NB, T * D])
        ffn = ExitStack()
        wl1 = sb("wl1", [P, TL, C * HID], FP, ffn)
        wl2 = sb("wl2", [HID + 1, TL, D + 1], FP, ffn)
        iota_b = sb("iota_b", [P, BLOCKS], FP, ffn)
        offs = sb("offs", [P, TREES, LEAVES], FP, ffn)
        tmp_p = sb("tmp_p", [P, NB * T, TL], FP, ffn)
        placef = sb("placef", [P, NB * T, TREES], FP, ffn)
        cmp_b = sb("cmp_b", [P, TREES, BLOCKS, LEAVES], FP, ffn)
        leaff = sb("leaff", [P, TREES * BLOCKS], FP, ffn)
        ffn.close()

        pidx = [sb(f"pidx{i}", [P, T * TREES], I32) for i in range(U)]
        k_all = xn2
        qr, kr, vr = ([sb(f"{n}{i}", [P, T, D]) for i in range(U)] for n in ("qr", "kr", "vr"))
        qT, kT = ([sb(f"{n}{i}", [P, C * S]) for i in range(2)] for n in ("qT", "kT"))
        pr = [sb(f"pr{i}", [P, T, S]) for i in range(2)]
        prT = [sb(f"prT{i}", [P, T, S]) for i in range(2)]
        m2, mb2, sum2, rsum2 = ([sb(f"{n}{i}", [P, T]) for i in range(2)]
                                for n in ("m2", "mb2", "sum2", "rsum2"))
        x1r = [sb(f"x1r{i}", [P, T, D]) for i in range(U)]
        res = [sb(f"res{i}", [P, T, D]) for i in range(U)]

        consts, weights, wt_late = sem("consts"), sem("weights"), sem("wt_late")
        x_in, c_in, xr_in = sems("x_in"), sems("c_in"), sems("xr_in")
        zeroed = sem("zeroed")
        (stats1, aggr1, var1, rstd1, xn_done, xnT_ps, xnT_sb, q_ps, qh_sb, ql_sb, k_ps, kh_sb, kl_sb,
         v_ps, v_sb, s_ps, max_sb, mT_ps, mh_sb, ml_sb, st_ps, exp_sb, sel_sb, pv_ps, nd_sb, ndT_ps, rden_sb, a_sb, aT_ps, aT_sb,
         wo_ps, x1_sb, stats2, aggr2, var2, rstd2, xn2_sb, xn2_kept, xn2T_ps, xn2T_sb, node_ps, sc_sb,
         g_step, lvl2, lvl3, oh_sb, oh_kept, rank_ps, rk_sb, rp_sb, rank_kept, count_up) = (
            sem(n) for n in
            ("stats1 aggr1 var1 rstd1 xn_done xnT_ps xnT_sb q_ps qh_sb ql_sb k_ps kh_sb kl_sb "
             "v_ps v_sb s_ps max_sb mT_ps mh_sb ml_sb st_ps exp_sb sel_sb pv_ps nd_sb ndT_ps rden_sb a_sb aT_ps aT_sb "
             "wo_ps x1_sb stats2 aggr2 var2 rstd2 xn2_sb xn2_kept xn2T_ps xn2T_sb node_ps sc_sb "
             "g_step lvl2 lvl3 oh_sb oh_kept rank_ps rk_sb rp_sb rank_kept count_up").split())
        stacked = [sems(f"stacked_r{r}_") for r in range(4)]
        unloaded = sems("unloaded")
        passed = sem("passed")
        m_row, k_ones = sem("m_row"), sem("k_ones")
        x1_out = sems("x1_out")
        route, iotas, placed, leaves = sem("route"), sem("iotas"), sem("placed"), sem("leaves")
        scat = sems("scat", TREES)
        (xbT_ps, xbT_sb, h_ps, h_sb, y_ps, y_sb, w_cp, hT_one) = (
            sem(n) for n in "xbT_ps xbT_sb h_ps h_sb y_ps y_sb w_cp hT_one".split())
        xb_in, y_out = sems("xb_in", UP), sems("y_out", UP)
        q_in, k_in = sem("q_in"), sem("k_in")
        qk_in, v_in = sems("qk_in", U), sems("v_in", U)
        (idx_cp, tq_ps, qT_sb, tk_ps, kT_sb, s2_ps, m2_sb, mb2_sb, e2_sb, rs2_sb, pT_ps, pT_sb, o_ps,
         res_sb) = (sem(n) for n in ("idx_cp tq_ps qT_sb tk_ps kT_sb s2_ps m2_sb mb2_sb e2_sb rs2_sb "
                                     "pT_ps pT_sb o_ps res_sb").split())
        x1r_in, r_out = sems("x1r_in", U), sems("r_out", U)

        def ge(eng, semaphore, value):
            if not isinstance(value, int) or value > 0:
                eng.wait_ge(semaphore, value)

        def apart(eng):
            eng.sem_inc(passed)

        def pipeline(step, eng):
            for b in range(-3, 6):
                step(b, b // 2, b % 2)
            with eng.Fori(3, NB // 2 - 2) as i:
                for u in range(2):
                    step(i * 2 + u, i, u)
            for b in range(NB - 4, NB + 3):
                step(b, b // 2, b % 2)

        def has(b, k):
            return not isinstance(b, int) or 0 <= b + k < NB

        def upto(b, k):
            return min(b + k + 1, NB) if isinstance(b, int) else b + (k + 1)

        def ge_edge(eng, semaphore, b, k):
            if isinstance(b, int):
                ge(eng, semaphore, upto(b, k))

        NCONST = 17
        S_BANKS, ST_BANKS, W_BANKS, G6, G7 = pairs[0], pairs[1], banks[4:6], banks[6], banks[7]
        block = ctx.enter_context(nc.Block())

        @block.sync
        def _(sp):
            def load_x(b, s):
                ge(sp, xn_done, T * (b - 1))
                sp.dma_start(xt[s][:], x[bass.ds(b * S, S), :].rearrange("(t p) d -> p t d", p=P)).then_inc(x_in[s], 16)

            def load_c(b, s):
                ge(sp, v_ps, b - 1)
                sp.dma_start(ct[s][:], ctxT[bass.ds(b * D, D), :].rearrange("(c p) k -> p c k", p=P)).then_inc(c_in[s], 16)

            def load_xr(b, s):
                ge(sp, x1_sb, b - 1)
                sp.dma_start(xr[s][:], x[bass.ds(b * S, S), :].rearrange("(t p) d -> p t d", p=P)).then_inc(xr_in[s], 16)

            def unload(b, n, s, m):
                hi, lo, hi_sem, lo_sem = ((q_hi, q_lo, qh_sb, ql_sb), (k_hi, k_lo, kh_sb, kl_sb))[m]
                if m == 0:
                    for r in range(4):
                        ge(sp, stacked[r][s], 16 * STACKS * n)
                sp.wait_ge(hi_sem, b + 1)
                sp.wait_ge(lo_sem, b + 1)
                for r, part in enumerate((hi, lo)):
                    sp.dma_start(parts_dram[s][m, :, r].rearrange("c p k -> p c k"), part[s][:].bitcast(FP)).then_inc(unloaded[s], 16)

            def stack(b, s, r, ms=(0, 1)):
                ge(sp, st_ps, PAIRS * (b - 2) + 2 * r + 2)
                c, par = r // HQ, r % HQ
                hs = slice(4 * r, 4 * r + 4)

                def rows(m, r0, r1):
                    return parts_dram[s][m, c, r0:r1].rearrange("r (d h e) k -> (r d) h e k", h=4, e=HQ)[:, :, par, :]

                for m, full, at_row, src in ((0, q4, 0, rows(0, 0, 2)), (0, q4, 2, rows(0, 1, 2)), (0, q4, 3, rows(0, 0, 1)),
                                             (1, k4, 0, rows(1, 0, 2)), (1, k4, 2, rows(1, 0, 2))):
                    if m in ms:
                        sp.dma_start(full[s][DK * at_row:DK * at_row + src.shape[0], hs, :].bitcast(FP), src).then_inc(stacked[r][s], 16)

            def step(b, n, u):
                early = isinstance(b, int) and b == -3
                if has(b, 3) and not early:
                    load_x(b + 3, 1 - u)
                if has(b, 1):
                    stack(b + 1, 1 - u, 2)
                if has(b, 1):
                    stack(b + 1, 1 - u, 3)
                if has(b, 2):
                    unload(b + 2, n + 1, u, 0)
                if has(b, 1):
                    k = ROWS // NB
                    for tree in range(TREES):
                        sp.dma_start(xs_dram[tree][bass.ds((b + 1) * k, k), :].rearrange("(p r) d -> p r d", p=P),
                                     zero[:].unsqueeze(1).to_broadcast([P, k // P, D])).then_inc(zeroed, 16)
                if has(b, -1):
                    load_xr(b - 1, 1 - u)
                if has(b, -2):
                    ge(sp, x1_sb, b - 1)
                    sp.dma_start(x1_dram[bass.ds((b - 2) * S, S), :].rearrange("(t p) d -> p t d", p=P),
                                 x1[u][:]).then_inc(x1_out[u], 16)
                if has(b, 2):
                    sp.wait_ge(unloaded[u], 64 * (n + 1) + 32)
                    unload(b + 2, n + 1, u, 1)
                    stack(b + 2, u, 0, ms=(0,))
                    sp.wait_ge(unloaded[u], 64 * (n + 2))
                    stack(b + 2, u, 0, ms=(1,))
                if has(b, 3) and not early:
                    load_c(b + 3, 1 - u)
                if has(b, 2):
                    stack(b + 2, u, 1)

            load_x(0, 0)
            load_c(0, 0)
            sp.wait_ge(consts, NCONST)
            pipeline(step, sp)

            sp.wait_ge(count_up, NB)
            sp.wait_ge(xn2_kept, NB)
            for s in range(2):
                sp.wait_ge(x1_out[s], 16 * (NB // 2))
            sp.wait_ge(zeroed, 16 * NB * TREES)
            for t in range(TREES):
                ts = slice(t * LEAVES, (t + 1) * LEAVES)
                sp.dma_start(wl1[:, ts, :], leafw1[t]).then_inc(wt_late, 16)
                sp.dma_start(wl2[:, ts, :], leafw2[t]).then_inc(wt_late, 16)

            def pair_rows(ap, g):
                return ap[bass.ds(g * RUN, 2 * RUN), :].rearrange("(o p) d -> p o d", p=P)

            def load_pair(tree, i, w):
                g = i * UB + 2 * w
                ge(sp, xbT_ps, g + 2 - UB)
                sp.dma_start(xb[w][:], pair_rows(xs_dram[tree], g - tree * BLOCKS)).then_inc(xb_in[w], 16)

            def store_pair(tree, i, w):
                g = i * UB + 2 * w
                sp.wait_ge(y_sb, g + 2)
                sp.dma_start(pair_rows(ys_dram[tree], g - tree * BLOCKS), yb[w][:]).then_inc(y_out[w], 16)

            K = BLOCKS // UB
            for tree in range(TREES):
                sp.wait_ge(scat[tree], 16 * NB * T)
                for w in range(UP):
                    load_pair(tree, tree * K, w)
                    if tree > 0:
                        store_pair(tree - 1, tree * K - 1, w)
                with sp.Fori(tree * K + 1, (tree + 1) * K) as i:
                    for w in range(UP):
                        load_pair(tree, i, w)
                        store_pair(tree, i - 1, w)
            for w in range(UP):
                store_pair(TREES - 1, TREES * K - 1, w)

            def rows(ap, b):
                return ap[bass.ds(b * S, S), :].rearrange("(t p) d -> p t d", p=P)

            def load_qk(i, u):
                b = i * U + u
                ge(sp, tq_ps, b - U + 1)
                ge(sp, tk_ps, b - U + 1)
                for dst, src in ((qr, q_all), (kr, k_all)):
                    sp.dma_start(dst[u][:].rearrange("p t d -> p (t d)"),
                                 src[:, bass.ds(b, 1), :].rearrange("p o n -> p (o n)")).then_inc(qk_in[u], 16)

            def load_x1r(i, u):
                b = i * U + u
                ge(sp, res_sb, T * (b - U + 1))
                sp.dma_start(x1r[u][:], rows(x1_dram, b)).then_inc(x1r_in[u], 16)

            def store_final(i, u):
                b = i * U + u
                sp.wait_ge(res_sb, T * (b + 1))
                sp.dma_start(rows(out, b), res[u][:]).then_inc(r_out[u], 16)

            sp.wait_ge(y_sb, TREES * BLOCKS)
            sp.wait_ge(q_in, 16 * NB * T)
            sp.wait_ge(k_in, 16 * NB * T)
            for u in range(U):
                load_qk(0, u)
                load_x1r(0, u)
            with sp.Fori(1, NB // U) as i:
                for u in range(U):
                    load_qk(i, u)
                    store_final(i - 1, u)
                    load_x1r(i, u)
            for u in range(U):
                store_final(NB // U - 1, u)
            for u in range(U):
                sp.wait_ge(r_out[u], 16 * (NB // U))
            sp.wait_ge(zeroed, 16 * NB * TREES)

        @block.tensor
        def _(pe):
            mm = nc.tensor.matmul

            def project(ps, w, actT):
                for o in range(C):
                    for c in range(C):
                        last = mm(ps[:, o * S:o * S + S], w[:, c, o * P:o * P + P], actT(c),
                                  start=(c == 0), stop=(c == C - 1))
                return last

            def scores(b, n, u, j):
                if j % 2 == 0:
                    pe.wait_ge(stacked[j // 2][1 - u], 16 * STACKS * (n + 1 + u))
                ge(pe, max_sb, PAIRS * (b + 1) + j)
                for e in range(2):
                    t, ps, q, k = 2 * j + e, S_BANKS[:, e, :], q4[1 - u], k4[1 - u]
                    mm(ps[:, 0:S], q[0:KS, t, P:S], k[0:KS, t, :], start=True, stop=False)
                    mm(ps[:, S:S + P], q[0:KS, t, 0:P], k[0:KS, t, 0:P], start=False, stop=False)
                for e in range(2):
                    last = mm(S_BANKS[:, e, P:S + P], identb[:], mask2[:], start=False, stop=True)
                last.then_inc(s_ps, 1)

            def scores_T(b, u, p):
                if p == 0:
                    pe.wait_ge(m_row, 32 * (b + 1))
                    if isinstance(b, int) and b in (0, 1):
                        pe.wait_ge(k_ones, b + 1)
                ge(pe, exp_sb, PAIRS * b + p)
                for e in range(2):
                    t, ps, q, k = 2 * p + e, ST_BANKS[:, e, :], q4[u], k4[u]
                    mm(ps[:, 0:S], k[0:KM, t, 0:P], q[0:KM, t, :], start=True, stop=True)
                    last = mm(ps[:, S:S + P], k[0:KM, t, P:S], q[0:KM, t, P:S], start=True, stop=True)
                last.then_inc(st_ps, 1)

            def weigh(b, u, r):
                c, par = r // HQ, r % HQ
                pe.wait_ge(sel_sb, PAIRS * b + 2 * r + 2)
                if r == 0:
                    pe.wait_ge(v_sb, b + 1)
                if r < HQ:
                    ge(pe, *((a_sb, HQ * (b - 1) + 1) if par == 0 else (aT_sb, b)))
                for kt in range(T):
                    for g in range(4):
                        t = 4 * r + g
                        last = mm(W_BANKS[par][32 * g:32 * g + 32, c * S + kt * P:c * S + S],
                                  vp[u][:, kt, HORDER[t], :],
                                  pt[:, t, 0:S] if kt == 0 else pt[:, t, S:S + P],
                                  start=(kt == 0), stop=(kt == 1))
                last.then_inc(pv_ps, 1)

            def rows_of(b, par):
                pe.wait_ge(nd_sb, HQ * (b - 1) + par + 1)
                for t in range(T):
                    for c in range(C):
                        last = nc.tensor.transpose(W_BANKS[par][:, (t * C + c) * P:(t * C + c) * P + P],
                                                   nd[par][:, c * S + t * P:c * S + t * P + P], ident[:])
                last.then_inc(ndT_ps, 1)

            def step(b, n, u):
                for j in range(PAIRS):
                    if has(b, 1):
                        scores(b, n, u, j)
                    if j >= LAG and has(b, 0):
                        scores_T(b, u, j - LAG)
                    if j < LAG and has(b, -1):
                        scores_T(b - 1, 1 - u, j + PAIRS - LAG)
                    if j == 6 and has(b, 0):
                        weigh(b, u, 0)
                    if j in (0, 2, 4) and has(b, -1):
                        weigh(b - 1, 1 - u, j // 2 + 1)
                    if j == 0 and has(b, 0):
                        pe.wait_ge(max_sb, PAIRS * (b + 1))
                        ge(pe, xnT_sb, upto(b, 2))
                        ge_edge(pe, sc_sb, b, -3)
                        for t in range(T):
                            last = nc.tensor.transpose(G6[0:NH, t * P:t * P + P], mneg[u][:, t, :], ident[:])
                        last.then_inc(mT_ps, 1)
                    if j == 1 and has(b, 2):
                        pe.wait_ge(xnT_sb, b + 3)
                        ge(pe, x1_sb, upto(b, -2))
                        ge_edge(pe, v_sb, b, 0)
                        ge_edge(pe, kl_sb, b, 1)
                        project(G7, wq, lambda c: xnT[:, c * S:c * S + S]).then_inc(q_ps, 1)
                    if j == 2 and has(b, -3):
                        pe.wait_ge(oh_sb, b - 2)
                        ge(pe, ml_sb, upto(b, 0))
                        o = oh[1 - u]
                        mm(G6[:, 128:128 + TL], trib[:], o[:, 0:TL], start=True, stop=True)
                        mm(G6[:, 192:192 + TL], trib[:], o[:, TL:2 * TL], start=True, stop=False)
                        mm(G6[:, 192:192 + TL], onesb[:], o[:, 0:TL], start=False, stop=True)
                        mm(G6[:, 256:256 + TL], onesb[:], o[:, 0:TL], start=True, stop=False)
                        mm(G6[:, 256:256 + TL], onesb[:], o[:, TL:2 * TL], start=False, stop=True
                           ).then_inc(rank_ps, 1)
                    if j == 3 and has(b, 2):
                        pe.wait_ge(c_in[u], 16 * (n + 2))
                        pe.wait_ge(qh_sb, b + 3)
                        pe.wait_ge(ql_sb, b + 3)
                        project(G7, wk, lambda c: ct[u][:, c, :]).then_inc(k_ps, 1)
                    if j == 3 and has(b, -1):
                        rows_of(b, 0)
                    if j == 4 and has(b, -2):
                        pe.wait_ge(xn2_sb, T * (b - 1))
                        ge(pe, rk_sb, upto(b, -3))
                        ge(pe, count_up, upto(b, -3))
                        ge_edge(pe, ml_sb, b, 0)
                        for t in range(T):
                            for c in range(C):
                                last = nc.tensor.transpose(G6[:, c * S + t * P:c * S + t * P + P],
                                                           xn2s[u][:, t, c * P:c * P + P], ident[:])
                        last.then_inc(xn2T_ps, 1)
                    if j == 5 and has(b, 1):
                        pe.wait_ge(c_in[1 - u], 16 * (n + 1 + u))
                        pe.wait_ge(kh_sb, upto(b, 2))
                        pe.wait_ge(kl_sb, upto(b, 2))
                        ge_edge(pe, x1_sb, b, -2)
                        for t in range(T):
                            for c in range(C):
                                last = mm(G7[:, t * D:t * D + D], ct[1 - u][:, c, t * P:t * P + P], wv[:, c, :],
                                          start=(c == 0), stop=(c == C - 1))
                        last.then_inc(v_ps, 1)
                    if j == 5 and has(b, -1):
                        rows_of(b, 1)
                    if j == 6 and has(b, -1):
                        pe.wait_ge(a_sb, HQ * b)
                        for t in range(T):
                            for c in range(C):
                                last = nc.tensor.transpose(W_BANKS[1][:, c * S + t * P:c * S + t * P + P],
                                                           arow[:, t, c * P:c * P + P], ident[:])
                        last.then_inc(aT_ps, 1)
                    if j == 6 and has(b, -2):
                        pe.wait_ge(xn2T_sb, b - 1)
                        for t in range(T):
                            for c in range(C):
                                last = mm(G6[:, t * 64:t * 64 + TREES * NODES], xn2T[:, c * S + t * P:c * S + t * P + P],
                                          ndT[:, c, :], start=(c == 0), stop=(c == C - 1))
                        last.then_inc(node_ps, 1)
                    if j == 7 and has(b, -1):
                        pe.wait_ge(aT_sb, b)
                        pe.wait_ge(v_sb, upto(b, 1))
                        ge_edge(pe, x1_sb, b, -2)
                        for t in range(T):
                            for c in range(C):
                                last = mm(G7[:, t * D:t * D + D], aT[:, c * S + t * P:c * S + t * P + P],
                                          wo[:, c, :], start=(c == 0), stop=(c == C - 1))
                        last.then_inc(wo_ps, 1)
                    if j == 7 and has(b, 3):
                        pe.wait_ge(xn_done, T * (b + 4))
                        ge(pe, sc_sb, upto(b, -2))
                        ge_edge(pe, ml_sb, b, 0)
                        ge_edge(pe, xnT_sb, b, 2)
                        for t in range(T):
                            for c in range(C):
                                last = nc.tensor.transpose(G6[:, c * S + t * P:c * S + t * P + P],
                                                           xn[1 - u][:, t, c * P:c * P + P], ident[:])
                        last.then_inc(xnT_ps, 1)

            pe.wait_ge(consts, NCONST)
            pe.wait_ge(weights, 16 * 7)
            pipeline(step, pe)

            G = TREES * BLOCKS

            def block_T(i, u):
                g = i * UB + u
                if u % 2 == 0:
                    pe.wait_ge(xb_in[u // 2], 16 * (i + 1))
                ge(pe, xbT_sb, g - 1)
                for c in range(C):
                    last = nc.tensor.transpose(banks[u % 2][:, c * P:c * P + P], xb[u // 2][:, u % 2, c * P:c * P + P], ident[:])
                last.then_inc(xbT_ps, 1)

            def block_h(i, u):
                g = i * UB + u
                pe.wait_ge(xbT_sb, g + 1)
                pe.wait_ge(w_cp, 2 * (g + 1))
                ge(pe, h_sb, g - 1)
                for c in range(C):
                    last = mm(banks[2 + u % 2][0:HID, 0:P], wb1[u][:, c * HID:c * HID + HID],
                              xbT[u % 2][:, c * P:c * P + P], start=(c == 0), stop=(c == C - 1))
                last.then_inc(h_ps, 1)

            def block_out(i, u):
                g = i * UB + u
                pe.wait_ge(h_sb, g + 1)
                ge(pe, y_sb, g - 1)
                mm(banks[4 + u % 2][:, 0:D], hT[u % 2][:], wb2[u][:, 0:D],
                   start=True, stop=True).then_inc(y_ps, 1)

            def blocks(i, more):
                for u in range(UB):
                    if u + 2 < UB or more:
                        block_T(i + (u + 2) // UB, (u + 2) % UB)
                    if u + 1 < UB or more:
                        block_h(i + (u + 1) // UB, (u + 1) % UB)
                    block_out(i, u)

            pe.wait_ge(hT_one, 2)
            block_T(0, 0)
            block_T(0, 1)
            block_h(0, 0)
            blocks(0, True)
            with pe.Fori(1, G // UB - 1) as i:
                blocks(i, True)
            blocks(G // UB - 1, False)

            pe.wait_ge(y_sb, G)

            def transposes(i, u):
                b = i * U + u
                pe.wait_ge(qk_in[u], 32 * (i + 1))
                for ps, src, done, free in ((banks[0], qr[u], tq_ps, qT_sb), (banks[1], kr[u], tk_ps, kT_sb)):
                    ge(pe, free, b)
                    for t in range(T):
                        for c in range(C):
                            last = nc.tensor.transpose(ps[:, c * S + t * P:c * S + t * P + P],
                                                       src[:, t, c * P:c * P + P], ident[:])
                    last.then_inc(done, 1)

            def scores(i, u):
                b, w = i * U + u, u % 2
                pe.wait_ge(qT_sb, b + 1)
                pe.wait_ge(kT_sb, b + 1)
                ge(pe, e2_sb, T * (b - 1))
                for t in range(T):
                    for c in range(C):
                        last = mm(banks[2 + w][:, t * S:t * S + S], qT[w][:, c * S + t * P:c * S + t * P + P],
                                  kT[w][:, c * S:c * S + S], start=(c == 0), stop=(c == C - 1))
                last.then_inc(s2_ps, 1)

            def probs_T(i, u):
                b, w = i * U + u, u % 2
                pe.wait_ge(e2_sb, T * (b + 1))
                ge(pe, pT_sb, b - 1)
                for qt in range(T):
                    for kt in range(T):
                        last = nc.tensor.transpose(banks[4 + w][:, kt * S + qt * P:kt * S + qt * P + P],
                                                   pr[w][:, qt, kt * P:kt * P + P], ident[:])
                last.then_inc(pT_ps, 1)

            def values(i, u):
                b, w = i * U + u, u % 2
                pe.wait_ge(pT_sb, b + 1)
                pe.wait_ge(v_in[u], 32 * (i + 1))
                ge(pe, res_sb, T * (b - 1))
                for t in range(T):
                    for kt in range(T):
                        last = mm(banks[6 + w][:, t * D:t * D + D], prT[w][:, kt, t * P:t * P + P], vr[u][:, kt, :],
                                  start=(kt == 0), stop=(kt == T - 1))
                last.then_inc(o_ps, 1)

            def finals(i, more):
                for u in range(U):
                    if u + 2 < U or more:
                        transposes(i + (u + 2) // U, (u + 2) % U)
                    probs_T(i, u)
                    if u + 1 < U or more:
                        scores(i + (u + 1) // U, (u + 1) % U)
                    values(i, u)

            transposes(0, 0)
            scores(0, 0)
            transposes(0, 1)
            finals(0, True)
            with pe.Fori(1, NB // U - 1) as i:
                finals(i, True)
            finals(NB // U - 1, False)

        @block.scalar
        def _(act):
            def exps(b, p):
                act.wait_ge(st_ps, PAIRS * b + p + 1)
                if p % 2 == 0:
                    ge(act, pv_ps, 4 * (b - 1) + p // 2 + 1)
                nc.scalar.activation(pt[:, 2 * p:2 * p + 2, :], ST_BANKS[:, :, 0:S + P], ACT.Exp,
                                     scale=SC).then_inc(exp_sb, 1)

            def weighed(b, par):
                act.wait_ge(pv_ps, 4 * (b - 1) + 3 + par)
                ge(act, ndT_ps, HQ * (b - 2) + par + 1)
                nc.scalar.copy(nd[par][:], W_BANKS[par][:]).then_inc(nd_sb, 1)

            def step(b, n, u):
                for j in range(PAIRS):
                    if j == 0 and has(b, 2):
                        act.wait_ge(xnT_ps, b + 3)
                        ge(act, q_ps, b + 2)
                        nc.scalar.copy(xnT[:], G6[:]).then_inc(xnT_sb, 1)
                    if j == 2 and has(b, 2):
                        act.wait_ge(q_ps, b + 3)
                        ge(act, unloaded[u], 64 * (n + 1))
                        nc.scalar.copy(q_hi[u][:].rearrange("p c k -> p (c k)"), G7[:]).then_inc(qh_sb, 1)
                    if j == 3 and has(b, -1):
                        weighed(b, 0)
                    if j == 7 and has(b, -1):
                        act.wait_ge(aT_ps, b)
                        ge(act, wo_ps, b - 1)
                        nc.scalar.copy(aT[:], W_BANKS[1][:]).then_inc(aT_sb, 1)
                    if j == 4 and has(b, 2):
                        act.wait_ge(k_ps, b + 3)
                        nc.scalar.copy(k_hi[u][:].rearrange("p c k -> p (c k)"), G7[:]).then_inc(kh_sb, 1)
                    if j == 4 and has(b, -2):
                        act.wait_ge(xn2_sb, T * (b - 1))
                        nc.scalar.copy(xn2[:, bass.ds(b - 2, 1), :],
                                       xn2s[u][:].rearrange("p t d -> p (t d)")).then_inc(xn2_kept, 1)
                    if j == 5 and has(b, -1):
                        weighed(b, 1)
                    if j == 5 and has(b, -2):
                        act.wait_ge(xn2T_ps, b - 1)
                        ge(act, node_ps, b - 2)
                        nc.scalar.copy(xn2T[:], G6[:]).then_inc(xn2T_sb, 1)
                    if j == 6 and has(b, 1):
                        act.wait_ge(v_ps, b + 2)
                        ge(act, pv_ps, 4 * b)
                        nc.scalar.copy(vp[1 - u][:].rearrange("p t h c -> p (t h) c")[:, :, 0:DK],
                                       G7[:].rearrange("p (m c) -> p m c", c=DK)).then_inc(v_sb, 1)
                    if j >= LAG and has(b, 0):
                        exps(b, j - LAG)
                    if j < LAG and has(b, -1):
                        exps(b - 1, j + PAIRS - LAG)
                    if j == 1 and has(b, 0):
                        act.wait_ge(mh_sb, b + 1)
                        act.wait_ge(ml_sb, b + 1)
                        ge(act, st_ps, PAIRS * (b - 1))
                        act.dma_start(q4[u][KS:KS + 1, :, :].bitcast(FP), m_hi[:].bitcast(FP)).then_inc(m_row, 16)
                        act.dma_start(q4[u][KS + 1:KS + 2, :, :].bitcast(FP), m_lo[:].bitcast(FP)).then_inc(m_row, 16)

            for dst, src in ((wq, wqT), (wk, wkT), (wv, wvT), (wo, woT)):
                act.dma_start(dst[:], src.rearrange("(c p) n -> p c n", p=P)).then_inc(weights, 16)
            act.dma_start(ndT[:], nodeT.rearrange("(c p) n -> p c n", p=P)).then_inc(weights, 16)
            for t in range(T):
                act.dma_start(ndb[:, t, :], nodeb.to_broadcast([P, TREES * NODES])).then_inc(weights, 16)
            pipeline(step, act)

            act.wait_ge(hT_one, 2)

            def copy_xT(i, u):
                g = i * UB + u
                act.wait_ge(xbT_ps, g + 1)
                ge(act, h_ps, g - 1)
                nc.scalar.copy(xbT[u % 2][:], banks[u % 2][:, 0:D]).then_inc(xbT_sb, 1)

            def relu(i, u):
                g = i * UB + u
                act.wait_ge(h_ps, g + 1)
                ge(act, y_ps, g - 1)
                nc.scalar.activation(hT[u % 2][0:HID, :], banks[2 + u % 2][0:HID, 0:P], ACT.Relu,
                                     bias=wb2[u][0:HID, D:D + 1]).then_inc(h_sb, 1)

            def copy_y(i, u):
                act.wait_ge(y_ps, i * UB + u + 1)
                ge(act, y_out[u // 2], 16 * i)
                nc.scalar.copy(yb[u // 2][:, u % 2, :], banks[4 + u % 2][:, 0:D]).then_inc(y_sb, 1)

            def blocks(i, after):
                for u in range(UB):
                    if u + 2 < UB or after:
                        copy_xT(i + (u + 2) // UB, (u + 2) % UB)
                    if u + 1 < UB or after:
                        relu(i + (u + 1) // UB, (u + 1) % UB)
                    copy_y(i, u)

            copy_xT(0, 0)
            copy_xT(0, 1)
            relu(0, 0)
            blocks(0, True)
            with act.Fori(1, TREES * BLOCKS // UB - 1) as i:
                blocks(i, True)
            blocks(TREES * BLOCKS // UB - 1, False)

            def copy_qT(i, u):
                b = i * U + u
                act.wait_ge(tq_ps, b + 1)
                ge(act, s2_ps, b - 1)
                nc.scalar.copy(qT[u % 2][:], banks[0][:]).then_inc(qT_sb, 1)

            def exps(i, u):
                b, w = i * U + u, u % 2
                act.wait_ge(mb2_sb, b + 1)
                ge(act, pT_ps, b - 1)
                ge(act, rs2_sb, b - 1)
                for t in range(T):
                    nc.scalar.activation(pr[w][:, t, :], banks[2 + w][:, t * S:t * S + S], ACT.Exp, scale=SC2,
                                         bias=mb2[w][:, t:t + 1], accum_out=sum2[w][:, t:t + 1]).then_inc(e2_sb, 1)

            def finals(i, more):
                for u in range(U):
                    if u + 2 < U or more:
                        copy_qT(i + (u + 2) // U, (u + 2) % U)
                    if u + 1 < U or more:
                        exps(i + (u + 1) // U, (u + 1) % U)

            copy_qT(0, 0)
            exps(0, 0)
            copy_qT(0, 1)
            finals(0, True)
            with act.Fori(1, NB // U - 1) as i:
                finals(i, True)
            finals(NB // U - 1, False)

        @block.vector
        def _(v):
            def norm_in(b, n, s):
                v.wait_ge(x_in[s], 16 * (n + 1))
                for t in range(T):
                    nc.vector.bn_stats(st1[:, t, :], xt[s][:, t, :]).then_inc(stats1, 1)
                v.wait_ge(stats1, T * (b + 1))
                ge(v, rstd1, b)
                apart(v)
                for t in range(T):
                    nc.vector.bn_aggr(mv1[:, t, :], st1[:, t, :]).then_inc(aggr1, 1)

            def norm_out(b, s):
                v.wait_ge(rstd1, b + 1)
                ge(v, xnT_ps, b - 1)
                for t in range(T):
                    nc.vector.tensor_scalar(xn[s][:, t, :], xt[s][:, t, :], mv1[:, t, 0:1], rs1[:, t:t + 1],
                                            ALU.subtract, ALU.mult).then_inc(xn_done, 1)

            def divide(b, par):
                v.wait_ge(ndT_ps, HQ * (b - 1) + par + 1)
                heads = W_BANKS[par][:].rearrange("p (m c) -> p m c", c=32)
                nc.vector.reciprocal(rden[par][:], heads[:, :, DK]).then_inc(rden_sb, 1)
                v.wait_ge(rden_sb, HQ * (b - 1) + par + 1)
                ge(v, aT_ps, b - 1)
                nc.vector.tensor_tensor(arow[:].rearrange("p t (m e c) -> p (t m) e c", e=HQ, c=DK)[:, :, par, :],
                                        heads[:, :, 0:DK],
                                        rden[par][:].unsqueeze(2).to_broadcast([P, T * C * 4, DK]),
                                        ALU.mult).then_inc(a_sb, 1)

            def low_part(b, u, hi, lo, hi_sem, lo_sem):
                v.wait_ge(hi_sem, b + 3)
                nc.vector.tensor_tensor(lo[u][:].rearrange("p c k -> p (c k)"), G7[:],
                                        hi[u][:].bitcast(FP).rearrange("p c k -> p (c k)"),
                                        ALU.subtract).then_inc(lo_sem, 1)

            def residual(b, n, u):
                v.wait_ge(wo_ps, b - 1)
                v.wait_ge(xr_in[u], 16 * n)
                ge(v, x1_out[u], 16 * (n - 1))
                ge(v, xn2_sb, T * (b - 2))
                nc.vector.tensor_tensor(x1[u][:].rearrange("p t d -> p (t d)"), G7[:],
                                        xr[u][:].rearrange("p t d -> p (t d)"), ALU.add).then_inc(x1_sb, 1)

            def residual_stats(b, u):
                v.wait_ge(x1_sb, b - 1)
                for t in range(T):
                    nc.vector.bn_stats(st2[:, t, :], x1[u][:, t, :]).then_inc(stats2, 1)
                v.wait_ge(stats2, T * (b - 1))
                ge(v, rstd2, b - 2)
                apart(v)
                for t in range(T):
                    nc.vector.bn_aggr(mv2[:, t, :], st2[:, t, :]).then_inc(aggr2, 1)

            def step(b, n, u):
                for j in range(PAIRS):
                    if j == 0 and has(b, -2):
                        residual(b, n, u)
                    if j == 6 and has(b, -1):
                        divide(b, 1)
                    if j == 7 and has(b, -2):
                        tree(b, n, u)
                    if has(b, 1):
                        v.wait_ge(s_ps, PAIRS * (b + 1) + j + 1)
                        if j == 0:
                            ge(v, mT_ps, b)
                        for t, cols in ((1, slice(0, S)), (0, slice(S, S + P))):
                            last = nc.vector.tensor_reduce(mneg[1 - u][:, t, 2 * j:2 * j + 2], S_BANKS[:, :, cols],
                                                           axis=AX.X, op=ALU.max, negate=True)
                        last.then_inc(max_sb, 1)
                    if j == 0 and has(b, -2):
                        residual_stats(b, u)
                    if j == 0 and has(b, 0):
                        v.wait_ge(mT_ps, b + 1)
                        ge(v, m_row, 32 * b)
                        nc.vector.tensor_copy(m_hi[:], G6[0:NH, 0:S]).then_inc(mh_sb, 1)
                        v.wait_ge(mh_sb, b + 1)
                        nc.vector.tensor_tensor(m_lo[:], G6[0:NH, 0:S], m_hi[:].bitcast(FP), ALU.subtract).then_inc(ml_sb, 1)
                    if j == 2 and has(b, 2):
                        low_part(b, u, q_hi, q_lo, qh_sb, ql_sb)
                    if j == 2 and has(b, -2):
                        v.wait_ge(rstd2, b - 1)
                        ge(v, xn2T_ps, b - 3)
                        ge(v, xn2_kept, b - 3)
                        for t in range(T):
                            nc.vector.tensor_scalar(xn2s[u][:, t, :], x1[u][:, t, :], mv2[:, t, 0:1],
                                                    rs2[:, t:t + 1], ALU.subtract, ALU.mult).then_inc(xn2_sb, 1)
                    if j == 3 and has(b, -3):
                        ranks(b, n, u)
                    if j == 3 and has(b, 3):
                        norm_in(b + 3, n + 1 + u, 1 - u)
                    if j == 4 and has(b, 2):
                        low_part(b, u, k_hi, k_lo, kh_sb, kl_sb)
                    if j == 4 and has(b, -1):
                        divide(b, 0)
                    if j == 5 and has(b, 3):
                        norm_out(b + 3, 1 - u)
                    if j == 5 and isinstance(b, int) and b in (-3, -2):
                        nc.vector.memset(k4[b + 3][KS:KM, :, :].bitcast(FP), 1.0).then_inc(k_ones, 1)
            def tree(b, n, u):
                v.wait_ge(node_ps, b - 1)
                nc.vector.tensor_tensor(sc[:], G6[:, 0:128].rearrange("p (t m) -> p t m", t=T)[:, :, 0:TREES * NODES],
                                        ndb[:], ALU.add).then_inc(sc_sb, 1)
                v.wait_ge(sc_sb, b - 1)
                scr = sc[:].rearrange("p t (r m) -> p (t r) m", m=NODES)
                nc.vector.tensor_scalar(g2[:, :, :, 1], scr, 0.0, None, ALU.is_ge).then_inc(g_step, 1)
                nc.vector.tensor_scalar(g2[:, :, :, 0], scr, 0.0, None, ALU.is_lt).then_inc(g_step, 1)
                v.wait_ge(g_step, 2 * (b - 1))
                R = T * TREES
                src = g2[:, :, 0, :]
                for lvl, (dst, done) in enumerate(((l2[:], lvl2), (l3[:], lvl3),
                                                   (oh[u][:].rearrange("p (r l) -> p r l", l=LEAVES), oh_sb))):
                    m = 2 << lvl
                    if done is oh_sb:
                        ge(v, oh_kept, b - 3)
                        ge(v, rank_ps, b - 3)
                        ge(v, rp_sb, b - 3)
                    nc.vector.tensor_tensor(dst.rearrange("p r (m e) -> p r m e", e=2),
                                            src.unsqueeze(3).to_broadcast([P, R, m, 2]),
                                            g2[:, :, m - 1:2 * m - 1, :], ALU.mult).then_inc(done, 1)
                    if done is not oh_sb:
                        v.wait_ge(done, b - 1)
                    src = dst

            def ranks(b, n, u):
                v.wait_ge(rank_ps, b - 2)
                ge(v, count_up, b - 3)
                ge(v, oh_sb, b - 2)
                nc.vector.tensor_tensor(rk[:], G6[:, 128:256].rearrange("p (t m) -> p t m", t=T)[:, :, 0:TL],
                                        count[:].unsqueeze(1).to_broadcast([P, T, TL]), ALU.add).then_inc(rk_sb, 1)
                v.wait_ge(rk_sb, b - 2)
                nc.vector.tensor_tensor(rp[:].rearrange("p t m -> p (t m)"), rk[:].rearrange("p t m -> p (t m)"),
                                        oh[1 - u][:], ALU.mult).then_inc(rp_sb, 1)
                nc.vector.tensor_tensor(count[:], count[:], G6[:, 256:256 + TL], ALU.add).then_inc(count_up, 1)
                v.wait_ge(rp_sb, b - 2)
                nc.vector.tensor_reduce(rank[:, bass.ds(b - 3, 1), :], rp[:].rearrange("p t (r l) -> p (t r) l", l=LEAVES),
                                        axis=AX.X, op=ALU.add).then_inc(rank_kept, 1)
                nc.vector.tensor_copy(onehot[:, bass.ds(b - 3, 1), :], oh[1 - u][:]).then_inc(oh_kept, 1)

            v.wait_ge(consts, NCONST)
            v.wait_ge(weights, 16 * 7)
            pipeline(step, v)

            steps = [0]

            def done(ins):
                steps[0] += 1
                ins.then_inc(route, 1)
                v.wait_ge(route, steps[0])

            v.wait_ge(count_up, NB)
            v.wait_ge(rank_kept, NB)
            v.wait_ge(oh_kept, NB)
            shift = RUN.bit_length() - 1
            done(nc.vector.tensor_scalar(count_i[0][:].rearrange("p r l -> p (r l)"), count[:], float(RUN - 1), None, ALU.add))
            done(nc.vector.tensor_scalar(count_i[1][:], count_i[0][:], shift, None, ALU.logical_shift_right))
            done(nc.vector.tensor_scalar(count_i[2][:], count_i[1][:], shift, None, ALU.logical_shift_left))
            done(nc.vector.tensor_copy(run[0][:, :, PAD:], count_i[2][:]))
            for k in range(4):
                w, a, o = 1 << k, run[k], run[k + 1]
                done(nc.vector.tensor_tensor(o[:, :, PAD:], a[:, :, PAD:], a[:, :, PAD - w:PAD - w + LEAVES], ALU.add))
            done(nc.vector.tensor_tensor(offs[:], run[4][:, :, PAD:], run[0][:, :, PAD:], ALU.subtract))
            for r in range(TREES):
                ls = slice(r * LEAVES, (r + 1) * LEAVES)
                done(nc.vector.tensor_tensor(tmp_p[:, :, ls], onehot[:].rearrange("p b (t m) -> p (b t) m", t=T)[:, :, ls],
                                             offs[:, r, :].unsqueeze(1).to_broadcast([P, NB * T, LEAVES]), ALU.mult))
                done(nc.vector.tensor_reduce(placef[:, :, r], tmp_p[:, :, ls], axis=AX.X, op=ALU.add))
                nc.vector.tensor_tensor(place[:].rearrange("p (t r) -> p t r", r=TREES)[:, :, r], placef[:, :, r],
                                        rank[:].rearrange("p b (t r) -> p (b t) r", r=TREES)[:, :, r],
                                        ALU.add).then_inc(placed, 1)
            v.wait_ge(iotas, 1)
            done(nc.vector.tensor_copy(iota_b[:], iota_i[:]))
            for r in range(TREES):
                last = nc.vector.tensor_tensor(cmp_b[:, r], iota_b[:].unsqueeze(2).to_broadcast([P, BLOCKS, LEAVES]),
                                               run[4][:, r, PAD:].unsqueeze(1).to_broadcast([P, BLOCKS, LEAVES]), ALU.is_ge)
                done(last)
            done(nc.vector.tensor_reduce(leaff[:], cmp_b[:].rearrange("p r b l -> p (r b) l"), axis=AX.X, op=ALU.add))
            for r in range(TREES):
                bs = slice(r * BLOCKS, (r + 1) * BLOCKS)
                last = nc.vector.tensor_scalar(blockleaf[:, bs], leaff[:, bs], float(LEAVES - 1), float(r * LEAVES),
                                               ALU.min, ALU.add)
            last.then_inc(leaves, 1)

            for u in range(2):
                nc.vector.memset(hT[u][HID:HID + 1, :], 1.0).then_inc(hT_one, 1)
            v.wait_ge(wt_late, 32 * TREES)
            v.wait_ge(leaves, 1)

            def take_weights(i, u):
                g = i * UB + u
                leaf = v.value_load(blockleaf[0:1, bass.ds(g, 1)], min_val=0, max_val=TL - 1)
                ge(v, y_ps, g - UB + 1)
                nc.vector.tensor_copy(wb1[u][:], wl1[:, bass.ds(leaf, 1), :].rearrange("p o n -> p (o n)")).then_inc(w_cp, 1)
                nc.vector.tensor_copy(wb2[u][:], wl2[:, bass.ds(leaf, 1), :].rearrange("p o n -> p (o n)")).then_inc(w_cp, 1)

            for u in range(UB):
                take_weights(0, u)
            with v.Fori(1, TREES * BLOCKS // UB) as i:
                for u in range(UB):
                    take_weights(i, u)

            def copy_kT(i, u):
                b = i * U + u
                v.wait_ge(tk_ps, b + 1)
                ge(v, s2_ps, b - 1)
                nc.vector.tensor_copy(kT[u % 2][:], banks[1][:]).then_inc(kT_sb, 1)

            def maxima(i, u):
                b, w = i * U + u, u % 2
                v.wait_ge(s2_ps, b + 1)
                nc.vector.tensor_reduce(m2[w][:], banks[2 + w][:].rearrange("p (t k) -> p t k", t=T), axis=AX.X,
                                        op=ALU.max, negate=True).then_inc(m2_sb, 1)
                v.wait_ge(m2_sb, b + 1)
                ge(v, e2_sb, T * (b - 1))
                nc.vector.tensor_scalar(mb2[w][:], m2[w][:], SC2, None, ALU.mult).then_inc(mb2_sb, 1)

            def copy_pT(i, u):
                b, w = i * U + u, u % 2
                v.wait_ge(pT_ps, b + 1)
                ge(v, o_ps, b - 1)
                nc.vector.tensor_copy(prT[w][:].rearrange("p t k -> p (t k)"), banks[4 + w][:]).then_inc(pT_sb, 1)
                nc.vector.reciprocal(rsum2[w][:], sum2[w][:]).then_inc(rs2_sb, 1)

            def finish(i, u):
                b, w = i * U + u, u % 2
                v.wait_ge(rs2_sb, b + 1)
                v.wait_ge(o_ps, b + 1)
                v.wait_ge(x1r_in[u], 16 * (i + 1))
                ge(v, r_out[u], 16 * i)
                for t in range(T):
                    nc.vector.scalar_tensor_tensor(res[u][:, t, :], banks[6 + w][:, t * D:t * D + D],
                                                   rsum2[w][:, t:t + 1], x1r[u][:, t, :],
                                                   ALU.mult, ALU.add).then_inc(res_sb, 1)

            def finals(i, more):
                for u in range(U):
                    if u + 2 < U or more:
                        copy_kT(i + (u + 2) // U, (u + 2) % U)
                    copy_pT(i, u)
                    if u + 1 < U or more:
                        maxima(i + (u + 1) // U, (u + 1) % U)
                    finish(i, u)

            copy_kT(0, 0)
            maxima(0, 0)
            copy_kT(0, 1)
            finals(0, True)
            with v.Fori(1, NB // U - 1) as i:
                finals(i, True)
            finals(NB // U - 1, False)

        @block.gpsimd
        def _(gp):
            pool = nc.gpsimd
            for tile, value in ((ident, 0.0), (mask2, 0.0), (trib, 1.0), (onesb, 1.0), (mhalf, -0.5), (zero, 0.0),
                                (count, 0.0), (vp[0], 1.0), (vp[1], 1.0), (run[0], 0.0), (run[1], 0.0),
                                (run[2], 0.0), (run[3], 0.0)):
                pool.memset(tile[:], value).then_inc(consts, 1)
            gp.wait_ge(consts, 13)
            pool.affine_select(out=ident[:], in_=ident[:], compare_op=ALU.not_equal, fill=1.0, base=0,
                               pattern=[[-1, P]], channel_multiplier=1).then_inc(consts, 1)
            m2v = mask2[:].rearrange("p (e k) -> p e k", e=2)
            pool.affine_select(out=m2v, in_=m2v, compare_op=ALU.is_ge, fill=NEG, base=0,
                               pattern=[[0, 2], [-1, P]], channel_multiplier=1).then_inc(consts, 1)
            pool.affine_select(out=trib[:], in_=trib[:], compare_op=ALU.is_gt, fill=0.0, base=0,
                               pattern=[[1, P]], channel_multiplier=-1).then_inc(consts, 1)
            gp.wait_ge(consts, 16)
            pool.tensor_copy(identb[:], ident[:]).then_inc(consts, 1)
            gp.wait_ge(consts, NCONST)

            def rsqrt(b, aggr, mv, ve, var_sem, rs, rstd_sem, prev_read):
                gp.wait_ge(aggr, T * (b + 1))
                ge(gp, *prev_read)
                apart(gp)
                pool.tensor_scalar(ve[:], mv[:, :, 1], EPS, None, ALU.add).then_inc(var_sem, 1)
                gp.wait_ge(var_sem, b + 1)
                pool.tensor_tensor(rs[:], ve[:], mhalf[:], ALU.pow).then_inc(rstd_sem, 1)

            def select(b, p):
                gp.wait_ge(exp_sb, PAIRS * b + p + 1)
                apart(gp)
                for cols in (slice(0, P), slice(S, S + P)):
                    dg = pt[:, 2 * p:2 * p + 2, cols]
                    last = pool.affine_select(out=dg, in_=dg, compare_op=ALU.is_ge, fill=0.0, base=0,
                                              pattern=[[0, 2], [1, P]], channel_multiplier=-1)
                last.then_inc(sel_sb, 1)

            def step(b, n, u):
                for j in range(PAIRS):
                    if j == 1 and has(b, -2):
                        rsqrt(b - 2, aggr2, mv2, ve2, var2, rs2, rstd2, (xn2_sb, T * (b - 2)))
                    if j == 4 and has(b, 3):
                        rsqrt(b + 3, aggr1, mv1, ve1, var1, rs1, rstd1, (xn_done, T * (b + 3)))
                    if j >= LAG and has(b, 0):
                        select(b, j - LAG)
                    if j < LAG and has(b, -1):
                        select(b - 1, j + PAIRS - LAG)

            pipeline(step, gp)

            gp.wait_ge(count_up, NB)
            for s in range(2):
                gp.wait_ge(x1_out[s], 16 * (NB // 2))
            pool.iota(iota_i[:], pattern=[[RUN, BLOCKS]], base=0, channel_multiplier=0).then_inc(iotas, 1)
            gp.wait_ge(zeroed, 16 * NB * TREES)
            gp.wait_ge(xn2_kept, NB)

            def scatter(tree):
                gp.wait_ge(placed, tree + 1)
                for t in range(NB * T):
                    k = t * TREES + tree
                    gp.indirect_dma_start(xs_dram[tree], bass.IndirectOffsetOnAxis(ap=place[:, k:k + 1], axis=0),
                                          xn2[:, t // T, (t % T) * D:(t % T) * D + D], None).then_inc(scat[tree], 16)

            for tree in range(TREES):
                scatter(tree)

            for tree, (rows_all, done) in enumerate(((q_all, q_in), (k_all, k_in))):
                for s in range(UP):
                    gp.wait_ge(y_out[s], 16 * (tree + 1) * BLOCKS // UB)
                if rows_all is xn2:
                    for s in range(TREES):
                        gp.wait_ge(scat[s], 16 * NB * T)
                for t in range(NB * T):
                    m = t * TREES + tree
                    gp.indirect_dma_start(rows_all[:, t // T, (t % T) * D:(t % T) * D + D], None, ys_dram[tree],
                                          bass.IndirectOffsetOnAxis(ap=place[:, m:m + 1], axis=0)).then_inc(done, 16)
            for s in range(UP):
                gp.wait_ge(y_out[s], 16 * TREES * BLOCKS // UB)

            def gather(i, u):
                b = i * U + u
                ge(gp, o_ps, b - U + 1)
                ge(gp, v_in[u], 32 * i)
                pool.tensor_copy(pidx[u][:], place[:, bass.ds(b * T * TREES, T * TREES)]).then_inc(idx_cp, 1)
                gp.wait_ge(idx_cp, b + 1)
                apart(gp)
                for t in range(T):
                    m = t * TREES + TREES - 1
                    gp.indirect_dma_start(vr[u][:, t, :], None, ys_dram[TREES - 1],
                                          bass.IndirectOffsetOnAxis(ap=pidx[u][:, m:m + 1], axis=0)
                                          ).then_inc(v_in[u], 16)

            for u in range(U):
                gather(0, u)
            with gp.Fori(1, NB // U) as i:
                for u in range(U):
                    gather(i, u)


def kernel(**a):
    import concourse.bacc as bacc
    from concourse.bass_utils import run_bass_kernel_spmd as run

    a = {k: np.asarray(v) for k, v in a.items()}
    n = {k: a[f"L0_xattn_{k}"] for k in ("w_q", "w_k", "w_v", "w_o")}
    f = {k: np.stack([a[f"L0_ffn_{t}_{k}"] for t in "qkv"]) for k in ("node_w", "node_b", "w1", "b1", "w2", "b2")}
    leafw1 = f["w1"].reshape(TREES, LEAVES, C, P, HID).transpose(0, 3, 1, 2, 4).reshape(TREES, P, LEAVES, C * HID)
    leafw2 = np.zeros((TREES, HID + 1, LEAVES, D + 1), np.float32)
    leafw2[:, 0:HID, :, 0:D] = f["w2"].transpose(0, 2, 1, 3)
    leafw2[:, HID, :, 0:D] = f["b2"]
    leafw2[:, 0:HID, :, D] = f["b1"].transpose(0, 2, 1)

    def by_dim(w):
        return w.reshape(D, C, NH // C, DK).transpose(0, 1, 3, 2).reshape(D, D)

    arrays = {
        "x": a["x"].reshape(NTOK, D),
        "ctxT": a["ctx_1024"].transpose(0, 2, 1).reshape(NB * D, S),
        "wqT": by_dim(n["w_q"].T), "wkT": by_dim(n["w_k"].T), "wvT": n["w_v"].T, "woT": n["w_o"].T,
        "nodeT": f["node_w"].reshape(TREES * NODES, D).T,
        "nodeb": f["node_b"].reshape(1, TREES * NODES),
        "leafw1": leafw1, "leafw2": leafw2,
    }
    arrays = {k: np.ascontiguousarray(v) for k, v in arrays.items()}
    nc = bacc.Bacc("TRN2", target_bir_lowering=False, num_devices=1)
    args = {k: nc.dram_tensor(k, v.shape, mybir.dt.from_np(v.dtype), kind="ExternalInput").ap()
            for k, v in arrays.items()}
    out = nc.dram_tensor("out", (NTOK, D), FP, kind="ExternalOutput").ap()
    build(nc, **args, out=out)
    r = run(nc, [arrays], core_ids=[0])
    return r.results[0]["out"].reshape(NB, S, D)
```
